# Optimizing a Trainium2 kernel written in Bass

```python
import numpy as np
import jax
import jax.numpy as jnp

def _softmax(x, axis=-1):
    return jax.nn.softmax(x, axis=axis)

def _gelu(x):
    return jax.nn.gelu(x, approximate=True)

def _silu(x):
    return jax.nn.silu(x)

def _sigmoid(x):
    return jax.nn.sigmoid(x)

def _layernorm(x, axis=-1, eps=1e-05):
    m = jnp.mean(x, axis=axis, keepdims=True)
    v = jnp.var(x, axis=axis, keepdims=True)
    return (x - m) / jnp.sqrt(v + eps)

def _scatter_add(tgt, idx, src, axis=0):
    return tgt.at[idx].add(src)

def _segment_sum(src, seg, n):
    return jax.ops.segment_sum(src, seg, n)
kernel_name = 'mk_gnn_preln_d1_gnn_r8_016087'

def setup_inputs(seed: int=0):
    np.random.seed(seed)
    _w = jnp.asarray

    def _rec_inputs():
        import jax
        import jax.numpy as jnp
        _gk = jax.random.key(seed)
        x = -0.000202 + 1 * jax.random.normal(jax.random.fold_in(_gk, 1), (6250, 128), jnp.float32)
        src = jax.random.randint(jax.random.fold_in(_gk, 2), (100000,), 0, 6250, jnp.int32)
        dst = jax.random.randint(jax.random.fold_in(_gk, 3), (100000,), 0, 6250, jnp.int32)
        _o = jnp.argsort(dst, stable=True)
        src = src[_o]
        dst = dst[_o]
        return (x, src, dst)
    x, src, dst = _rec_inputs()

    def _L0_gnn_setup():
        import jax, jax.numpy as jnp
        import numpy as np
        N_NODES = 6250
        N_EDGES = 75000
        D_IN = 128
        D_OUT = 128
        key = jax.random.key(seed)
        k1, k2, k3, k4 = jax.random.split(key, 4)
        x = jax.random.normal(k1, (N_NODES, D_IN), dtype=jnp.float32)
        edge_index = jax.random.randint(k2, (2, N_EDGES), 0, N_NODES, dtype=jnp.int64)
        W1 = jax.random.normal(k3, (2 * D_IN, D_OUT), dtype=jnp.float32) * (1.0 / np.sqrt(2 * D_IN))
        b1 = jnp.zeros((D_OUT,), dtype=jnp.float32)
        W2 = jax.random.normal(k4, (D_OUT, D_OUT), dtype=jnp.float32) * (1.0 / np.sqrt(D_OUT))
        b2 = jnp.zeros((D_OUT,), dtype=jnp.float32)
        return {'x': x, 'edge_index': edge_index, 'W1': W1, 'b1': b1, 'W2': W2, 'b2': b2}
    _L0_gnn_all = _L0_gnn_setup()
    _L0_gnn_in = {k: v for k, v in _L0_gnn_all.items() if k in ('W1', 'b1', 'W2', 'b2')}
    del _L0_gnn_all
    return {'x': x, 'src': src, 'dst': dst, 'L0_gnn_W1': _L0_gnn_in['W1'], 'L0_gnn_b1': _L0_gnn_in['b1'], 'L0_gnn_W2': _L0_gnn_in['W2'], 'L0_gnn_b2': _L0_gnn_in['b2']}

def reference(x, src, dst, L0_gnn_W1, L0_gnn_b1, L0_gnn_W2, L0_gnn_b2):
    import jax
    import jax.numpy as jnp

    def _L0_gnn_ref(x, edge_index, W1, b1, W2, b2):
        import jax, jax.numpy as jnp
        import numpy as np
        N_NODES = 6250
        N_EDGES = 75000
        D_IN = 128
        D_OUT = 128
        row, col = (edge_index[0], edge_index[1])
        x_col = x[col]
        feat = jnp.concatenate([x_col, x[row] - x_col], axis=-1)
        h = jax.nn.relu(feat @ W1 + b1)
        messages = h @ W2 + b2
        out = jax.ops.segment_max(messages, col, num_segments=x.shape[0])
        out = jnp.where(jnp.isneginf(out), jnp.zeros_like(out), out)
        return out
    edge_index = jnp.stack([src, dst])
    h = jnp.maximum(_layernorm(x, axis=-1), 0.0)
    x = x + _L0_gnn_ref(h, edge_index, L0_gnn_W1, L0_gnn_b1, L0_gnn_W2, L0_gnn_b2)
    return x

_drawn_inputs = setup_inputs


def setup_inputs(seed=0):
    import zlib

    import numpy as np

    out = dict(_drawn_inputs(seed))
    spreads = {'L0_gnn_b1': (0.0, 0.1), 'L0_gnn_b2': (0.0, 0.1)}
    factors = {}
    for name, (base, spread) in spreads.items():
        noise = np.random.default_rng([zlib.crc32(name.encode()), seed]).standard_normal(out[name].shape)
        drawn = base * np.exp(spread * noise) if base else spread * noise
        out[name] = jnp.asarray(drawn.astype(out[name].dtype))
    for name, factor in factors.items():
        out[name] = (out[name] * factor).astype(out[name].dtype)
    return out
```

```python
from contextlib import ExitStack

import concourse.bass as bass
from concourse import mybir


def gnn_kernel(nc, x, src, dst, w1, b1, w2, b2, out):
    f32, bf16, i32 = mybir.dt.float32, mybir.dt.bfloat16, mybir.dt.int32
    ALU, ACT, AX = mybir.AluOpType, mybir.ActivationFunctionType, mybir.AxisListType

    N, F = x.shape
    E = src.shape[0]
    P = 128
    GE = 512
    GT_ = GE // P
    U = 4
    RE = U * GE
    R = -(-E // RE)
    NG = R * U
    E_FULL = (R - 1) * RE
    E_TAIL = E - E_FULL
    NT = -(-N // P)
    N_FULL = (NT - 1) * P
    N_TAIL = N - N_FULL
    BT = 4
    NB = -(-NT // BT)
    assert NT == (NB - 1) * BT + 1 and (NB - 1) % 2 == 0 and 0 < E_TAIL < RE and N_TAIL > 0
    NPAD = (NT + 1) * P
    NO_NODE = N
    WIDE_OFF = 1024.0
    NO_SCATTER = 20000.0
    PENALTY = -3.0e38
    EPS = 1e-5
    LAG = 4

    q_table = nc.dram_tensor("q_table", (N, F), f32, kind="Internal").ap()
    p_table = nc.dram_tensor("p_table", (NPAD, F), f32, kind="Internal").ap()
    rows_dram = nc.dram_tensor("rows_dram", (R, U * 2 * GE), bf16, kind="Internal").ap()
    p_index = nc.dram_tensor("p_index", (R, RE), i32, kind="Internal").ap()
    s_index = nc.dram_tensor("s_index", (R, RE), i32, kind="Internal").ap()
    wide_out = nc.dram_tensor("wide_out", (NT * P, F), f32, kind="Internal").ap()

    ctx = ExitStack()
    with ctx:
        def sb(name, shape, dt):
            return ctx.enter_context(nc.sbuf_tensor(name, shape, dt))

        def sem(name):
            return ctx.enter_context(nc.semaphore(name))

        ident = sb("ident", [P, P], f32)
        ones_row = sb("ones_row", [1, P], bf16)
        iota_part_i = sb("iota_part_i", [P, 1], i32)
        iota_part = sb("iota_part", [P, 1], f32)
        iota_free_i = sb("iota_free_i", [P, P], i32)
        iota_free1 = sb("iota_free1", [P, P], f32)
        eps_col = sb("eps_col", [P, 1], f32)
        w1_sb = sb("w1_sb", [P, 2, F], f32)
        w1_diff = sb("w1_diff", [P, F], f32)
        w2_sb = sb("w2_sb", [P, F], f32)
        b1_col = sb("b1_col", [P, 1], f32)
        b2_col = sb("b2_col", [P, 1], f32)
        zeros = sb("zeros", [P, F], f32)
        x_sb = sb("x_sb", [P, NT, F], f32)
        stats = sb("stats", [P, 2, BT, 6], f32)
        mean_var = sb("mean_var", [P, 2, BT, 2], f32)
        std = sb("std", [P, 2, BT], f32)
        rstd = sb("rstd", [P, 2, BT], f32)
        neg_mean = sb("neg_mean", [P, 2, BT], f32)
        h_sb = sb("h_sb", [P, 2, BT, F], f32)
        hT_sb = sb("hT_sb", [P, 2, BT, P], f32)
        p_rows = sb("p_rows", [P, 2, BT, F], f32)
        q_rows = sb("q_rows", [P, 2, BT, F], f32)
        outT = sb("outT", [P, NPAD], f32)
        outT_block = sb("outT_block", [P, 2, BT * P], f32)
        src_row = sb("src_row", [R, RE], i32)
        src_row_f = sb("src_row_f", [R, RE], f32)
        dst_row = sb("dst_row", [R, U, GE], i32)
        dst_next = sb("dst_next", [R, U, GE], i32)
        dst_before = sb("dst_before", [R, 1], i32)
        rel_i = sb("rel_i", [R, U, GE], i32)
        last = sb("last", [R, RE], f32)
        wide = sb("wide", [R, U], f32)
        wide_off = sb("wide_off", [R, U], f32)
        rel_last = sb("rel_last", [R, RE], f32)
        start = sb("start", [R, RE], f32)
        rowpack = sb("rowpack", [R, U, 2, GE], bf16)
        base_row = sb("base_row", [1, NG], i32)
        end_row = sb("end_row", [1, NG], i32)
        wide_row = sb("wide_row", [1, NG], f32)
        any_wide_i = sb("any_wide_i", [1, 1], i32)
        src_col = sb("src_col", [P, R, U * GT_], i32)
        rel_last_col = sb("rel_last_col", [P, R, U * GT_], f32)
        idx = sb("idx", [P, U, GT_], i32)
        G = sb("G", [P, U, GT_, F], f32)
        p_win = sb("p_win", [P, U, F], f32)
        rowbuf = sb("rowbuf", [1, U, 2, GE], bf16)
        onehot = sb("onehot", [P, 2, GE], f32)
        px_sb = sb("px_sb", [P, 2, GE], f32)
        H = sb("H", [P, 2, GE], f32)
        M = sb("M", [P, 2, GE], f32)
        S = sb("S", [P, 2, GE], f32)
        L = sb("L", [P, 2, GT_, P], f32)
        ST = sb("ST", [P, U, GT_, F], f32)
        idx_p = sb("idx_p", [P, U, GT_], i32)
        idx_s = sb("idx_s", [P, U, GT_], i32)

        bank = [ctx.enter_context(nc.psum_tensor(f"bank{i}", [P, GE], f32)) for i in range(8)]
        hT_ps, p_ps, q_ps = bank[0:2], bank[2:4], bank[4:6]
        col_ps = bank[6:8]
        GT_ps, PX_ps, rel_ps, pen_ps, M_ps, ST_ps, sel_ps = bank[0:7]
        fin_ps = bank[0:2]

        S_ = {n: sem(n) for n in """
            dve_init pool_init ident_ready weights_in wdiff_ready
            src_in dst_in dstn_in before_in before_main edges_memset base_in bias_in
            x_first x_rest x_tail
            stats_done mv_done sqrt_done rstd_done nm_done relu_done transp_done hT_done pq_done q_evac p_evac
            q_stored0 q_stored1 p_stored0 p_stored1 p_zero
            src_f_ready src_T src_col_ready rel_i_ready last_ready wide_ready woff_ready
            rel_row_ready rel_last_ready start_ready pen_ready rel_T rel_col_ready rows_stored anyw_ready dve_small
            idx_staged rel_done onehot_done gt_done px_done px_evac gates sum_done hidden_done m_done m_evac
            pen_done scan_done st_done st_evac L_done sel_done acc_done
            released wide_merged fin_copied fin_T fin_added out_stored outT_zero
            slow_v slow_store slow_idx slow_gather slow_scatter slow_zero
            """.split()}
        gathered = [sem(f"gathered{c}") for c in range(U)]
        win_in = [sem(f"win_in{c}") for c in range(U)]
        row_in = [sem(f"row_in{c}") for c in range(U)]

        def wait(eng, name, value, least):
            if least > 0:
                eng.wait_ge(S_[name] if isinstance(name, str) else name, value)

        def gate(eng):
            eng.sem_inc(S_["gates"], 1)

        T_FIRST, T_BODY, T_END = 6, NB - 1, NB + 3
        X_FIRST = 4
        G_FIRST, G_BODY, G_END = U, NG, NG + 3

        def tiles_of(least):
            return 1 if least == NB - 1 else BT

        block = ctx.enter_context(nc.Block())

        @block.sync
        def _(sp):
            sp.wait_ge(S_["edges_memset"], 5)
            src_full = src[0:E_FULL].rearrange("(r e) -> r e", e=RE)
            src_tail = src[E_FULL:E].rearrange("(r e) -> r e", r=1)
            sp.dma_start(src_row[0:R - 1, :], src_full).then_inc(S_["src_in"], 16)
            sp.dma_start(src_row[R - 1:R, 0:E_TAIL], src_tail).then_inc(S_["src_in"], 16)
            tiles = x[0:N_FULL, :].rearrange("(t p) f -> p t f", p=P)
            half = X_FIRST * BT
            sp.dma_start(x_sb[:, 0:half, :], tiles[:, 0:half, :]).then_inc(S_["x_first"], 16)
            sp.dma_start(w1_sb[:, :, :], w1.rearrange("(a k) f -> k a f", a=2)).then_inc(S_["weights_in"], 16)
            sp.dma_start(x_sb[:, half:NT - 1, :], tiles[:, half:NT - 1, :]).then_inc(S_["x_rest"], 16)
            sp.dma_start(x_sb[0:N_TAIL, NT - 1, :], x[N_FULL:N, :]).then_inc(S_["x_tail"], 16)
            dst_full = dst[0:E_FULL].rearrange("(r e) -> r e", e=RE)
            dst_tail = dst[E_FULL:E].rearrange("(r e) -> r e", r=1)
            dst_flat = dst_row[:, :, :].rearrange("r u e -> r (u e)")
            sp.dma_start(dst_flat[0:R - 1, :], dst_full).then_inc(S_["dst_in"], 16)
            sp.dma_start(dst_flat[R - 1:R, 0:E_TAIL], dst_tail).then_inc(S_["dst_in"], 16)
            next_flat = dst_next[:, :, :].rearrange("r u e -> r (u e)")
            sp.dma_start(next_flat[0:R - 1, :], dst[1:E_FULL + 1].rearrange("(r e) -> r e", e=RE)).then_inc(S_["dstn_in"], 16)
            sp.dma_start(next_flat[R - 1:R, 0:E_TAIL - 1],
                         dst[E_FULL + 1:E].rearrange("(r e) -> r e", r=1)).then_inc(S_["dstn_in"], 16)
            sp.dma_start(w2_sb[:, :], w2).then_inc(S_["bias_in"], 16)
            sp.dma_start(b1_col[:, :], b1.rearrange("(k a) -> k a", a=1)).then_inc(S_["bias_in"], 16)
            sp.dma_start(b2_col[:, :], b2.rearrange("(k a) -> k a", a=1)).then_inc(S_["bias_in"], 16)
            with nc.allow_non_contiguous_dma(reason="one number of each group or row"):
                sp.dma_start(dst_before[1:R, :], bass.AP(dst.tensor, RE - 1, [[RE, R - 1], [1, 1]])).then_inc(S_["before_in"], 16)
                sp.dma_start(base_row[:, :], bass.AP(dst.tensor, 0, [[GE * NG, 1], [GE, NG]])).then_inc(S_["base_in"], 16)
                sp.dma_start(end_row[:, 0:NG - 1], bass.AP(dst.tensor, GE - 1, [[GE * NG, 1], [GE, NG - 1]])).then_inc(S_["base_in"], 16)
            sp.wait_ge(S_["pool_init"], 1)
            sp.dma_start(p_table[N:N_FULL + P, :], zeros[0:P - N_TAIL, :]).then_inc(S_["p_zero"], 16)
            sp.dma_start(p_table[N_FULL + P:NPAD, :], zeros[:, :]).then_inc(S_["p_zero"], 16)

            def store_tables(b, par):
                rows = (b * BT) * P if isinstance(b, int) else b * (BT * P)
                sp.wait_ge(S_["q_evac"], b + 1)
                sp.dma_start(q_table[bass.ds(rows, BT * P), :].rearrange("(t p) f -> p t f", p=P),
                             q_rows[:, par, :, :]).then_inc(S_[f"q_stored{par}"], 16)
                sp.wait_ge(S_["p_evac"], b + 1)
                sp.dma_start(p_table[bass.ds(rows, BT * P), :].rearrange("(t p) f -> p t f", p=P),
                             p_rows[:, par, :, :]).then_inc(S_[f"p_stored{par}"], 16)

            with sp.Fori(0, (NB - 1) // 2) as i:
                for par in range(2):
                    store_tables(i * 2 + par, par)
            sp.wait_ge(S_["q_evac"], NB)
            sp.dma_start(q_table[N_FULL:N, :], q_rows[0:N_TAIL, 0, 0, :]).then_inc(S_["q_stored0"], 16)
            sp.wait_ge(S_["p_evac"], NB)
            sp.dma_start(p_table[N_FULL:N, :], p_rows[0:N_TAIL, 0, 0, :]).then_inc(S_["p_stored0"], 16)

            sp.wait_ge(S_["rel_row_ready"], 1)
            sp.wait_ge(S_["pen_ready"], 1)
            sp.dma_start(rows_dram[:, :], rowpack[:, :, :, :].rearrange("r u a e -> r (u a e)")).then_inc(S_["rows_stored"], 16)
            sp.wait_ge(S_["p_zero"], 32)
            sp.wait_ge(S_["p_stored0"], 16 * ((NB - 1) // 2 + 1))
            sp.wait_ge(S_["p_stored1"], 16 * ((NB - 1) // 2))
            sp.wait_ge(S_["base_in"], 32)
            sp.wait_ge(S_["rows_stored"], 16)
            rows_by_turn = rows_dram.rearrange("r (u c) -> r u c", u=U)

            def load_group(i, c, again):
                j = i * U + c
                if again:
                    sp.wait_ge(S_["px_done"], i * U + (c - U + 1))
                base = sp.value_load(base_row[0:1, bass.ds(j, 1)], min_val=0, max_val=N - 1)
                sp.dma_start(p_win[:, c, :], p_table[bass.ds(base, P), :]).then_inc(win_in[c], 16)
                if again:
                    sp.wait_ge(S_["pen_done"], i * U + (c - U + 1))
                sp.dma_start(rowbuf[0:1, c, :, :].rearrange("o a e -> o (a e)"),
                             rows_by_turn[bass.ds(i, 1), c, :]).then_inc(row_in[c], 16)

            for c in range(U):
                load_group(0, c, False)
            with sp.Fori(1, R) as i:
                for c in range(U):
                    load_group(i, c, True)

            out_tiles = out[0:N_FULL, :].rearrange("(t p) f -> p t f", p=P)
            with sp.Fori(0, NB - 1) as b:
                sp.wait_ge(S_["fin_added"], b + 1)
                sp.dma_start(out[bass.ds(b * (BT * P), BT * P), :].rearrange("(t p) f -> p t f", p=P),
                             x_sb[:, bass.ds(b * BT, BT), :]).then_inc(S_["out_stored"], 16)
            sp.wait_ge(S_["fin_added"], NB)
            sp.dma_start(out[N_FULL:N, :], x_sb[0:N_TAIL, NT - 1, :]).then_inc(S_["out_stored"], 16)
            sp.wait_ge(S_["out_stored"], 16 * NB)

        @block.gpsimd
        def _(pool):
            pool.memset(zeros[:, :], 0.0).then_inc(S_["pool_init"], 1)
            pool.memset(ident[:, :], 0.0).then_inc(S_["pool_init"], 1)
            pool.iota(iota_part_i[:, :], pattern=[[0, 1]], base=0, channel_multiplier=1).then_inc(S_["pool_init"], 1)
            pool.iota(iota_free_i[:, :], pattern=[[1, P]], base=1, channel_multiplier=0).then_inc(S_["pool_init"], 1)
            pool.wait_ge(S_["pool_init"], 2)
            pool.affine_select(out=ident[:, :], in_=ident[:, :], compare_op=ALU.not_equal, fill=1.0, base=0,
                               pattern=[[-1, P]], channel_multiplier=1).then_inc(S_["ident_ready"], 1)
            pool.memset(outT[:, :], 0.0).then_inc(S_["outT_zero"], 1)
            pool.wait_ge(S_["src_in"], 32)
            pool.tensor_copy(src_row_f[:, :], src_row[:, :]).then_inc(S_["src_f_ready"], 1)
            pool.wait_ge(S_["dst_in"], 32)
            pool.tensor_tensor(rel_i[:, :, :], dst_row[:, :, :], dst_row[:, :, 0:1].to_broadcast([R, U, GE]),
                               ALU.subtract).then_inc(S_["rel_i_ready"], 1)
            pool.wait_ge(S_["anyw_ready"], 1)
            any_wide = pool.value_load(any_wide_i[0:1, 0:1], min_val=0, max_val=1)
            pool.wait_ge(S_["q_stored0"], 16 * ((NB - 1) // 2 + 1))
            pool.wait_ge(S_["q_stored1"], 16 * ((NB - 1) // 2))

            def gather(i, c, again, signal):
                pool.wait_ge(S_["idx_staged"], i * U + (c + 1))
                if again:
                    pool.wait_ge(S_["gt_done"], i * U + (c - U + 1))
                gate(pool)
                for t in range(GT_):
                    pool.indirect_dma_start(G[:, c, t, :], None, q_table[:, :],
                                            bass.IndirectOffsetOnAxis(ap=idx[:, c, t:t + 1], axis=0)).then_inc(signal, 16)

            def slow_setup():
                v = [0]

                def chain(instruction):
                    v[0] += 1
                    instruction.then_inc(S_["slow_v"], 1)
                    pool.wait_ge(S_["slow_v"], v[0])

                pool.dma_start(wide_out.rearrange("(t p) f -> p t f", p=P),
                               zeros[:, :].rearrange("p (a f) -> p a f", a=1).to_broadcast([P, NT, F])).then_inc(S_["slow_zero"], 16)
                pool.wait_ge(S_["src_T"], 2)
                d, a = src_row_f, src_row
                by_group = lambda t: t[:, :].rearrange("r (u e) -> r u e", u=U)
                spread = wide[:, :].rearrange("r (u o) -> r u o", o=1).to_broadcast([R, U, GE])
                chain(pool.tensor_copy(d[:, :], dst_row[:, :, :].rearrange("r u e -> r (u e)")))
                chain(pool.tensor_scalar(d[:, :], d[:, :], -float(NO_NODE), None, ALU.add))
                chain(pool.tensor_tensor(by_group(d), by_group(d), spread, ALU.mult))
                chain(pool.tensor_scalar(a[:, :], d[:, :], float(NO_NODE), None, ALU.add))
                pool.dma_start(p_index[:, :], a[:, :]).then_inc(S_["slow_store"], 16)
                pool.wait_ge(S_["slow_store"], 16)
                chain(pool.tensor_copy(d[:, :], dst_row[:, :, :].rearrange("r u e -> r (u e)")))
                chain(pool.tensor_scalar(d[:, :], d[:, :], -NO_SCATTER, None, ALU.add))
                chain(pool.tensor_tensor(by_group(d), by_group(d), spread, ALU.mult))
                pool.wait_ge(S_["last_ready"], 1)
                chain(pool.tensor_tensor(d[:, :], d[:, :], last[:, :], ALU.mult))
                chain(pool.tensor_scalar(a[:, :], d[:, :], NO_SCATTER, None, ALU.add))
                pool.dma_start(s_index[:, :], a[:, :]).then_inc(S_["slow_store"], 16)
                pool.wait_ge(S_["slow_store"], 32)
                pool.wait_ge(S_["slow_zero"], 16)
                pool.wait_ge(S_["p_zero"], 32)
                pool.wait_ge(S_["p_stored0"], 16 * ((NB - 1) // 2 + 1))
                pool.wait_ge(S_["p_stored1"], 16 * ((NB - 1) // 2))

            p_cols = p_index.rearrange("r (u t p) -> p (r u) t", p=P, t=GT_)
            s_cols = s_index.rearrange("r (u t p) -> p (r u) t", p=P, t=GT_)

            def slow_gather(i, c, again):
                j = i * U + c
                if again:
                    pool.wait_ge(S_["slow_scatter"], (j - (U - 1)) * (16 * GT_))
                with nc.allow_non_contiguous_dma(reason="an index per partition"):
                    gate(pool)
                    pool.dma_start(idx_p[:, c, :].rearrange("p (o t) -> p o t", o=1),
                                   p_cols[:, bass.ds(j, 1), :]).then_inc(S_["slow_idx"], 16)
                    pool.wait_ge(S_["slow_idx"], (j * 2 + 1) * 16)
                    gate(pool)
                    pool.dma_start(idx_s[:, c, :].rearrange("p (o t) -> p o t", o=1),
                                   s_cols[:, bass.ds(j, 1), :]).then_inc(S_["slow_idx"], 16)
                    pool.wait_ge(S_["slow_idx"], (j * 2 + 2) * 16)
                gather(i, c, again, S_["slow_gather"])
                pool.wait_ge(S_["slow_gather"], (j + 1) * (16 * GT_))
                gate(pool)
                for t in range(GT_):
                    pool.indirect_dma_start(G[:, c, t, :], None, p_table[:, :],
                                            bass.IndirectOffsetOnAxis(ap=idx_p[:, c, t:t + 1], axis=0),
                                            compute_op=ALU.add).then_inc(gathered[c], 16)

            def slow_scatter(i, c):
                j = i * U + c
                pool.wait_ge(S_["st_evac"], j + 1)
                gate(pool)
                for t in range(GT_):
                    pool.indirect_dma_start(wide_out[:, :], bass.IndirectOffsetOnAxis(ap=idx_s[:, c, t:t + 1], axis=0),
                                            ST[:, c, t, :], None, bounds_check=N - 1, oob_is_err=False
                                            ).then_inc(S_["slow_scatter"], 16)
                pool.wait_ge(S_["slow_scatter"], (j + 1) * (16 * GT_))
                pool.sem_inc(S_["released"], 1)

            pool.sem_inc(S_["released"], U)
            with pool.If(any_wide > 0):
                slow_setup()
                for c in range(U):
                    slow_gather(0, c, False)
                with pool.Fori(1, R) as i:
                    for c in range(U):
                        slow_scatter(i - 1, c)
                        slow_gather(i, c, True)
                for c in range(U):
                    slow_scatter(R - 1, c)
                pool.dma_start(x_sb[:, :, :], wide_out.rearrange("(t p) f -> p t f", p=P),
                               accum_op=ALU.add).then_inc(S_["slow_zero"], 16)
                pool.wait_ge(S_["slow_zero"], 32)
                pool.sem_inc(S_["wide_merged"], 1)
            with pool.Else():
                pool.sem_inc(S_["released"], NG)
                for c in range(U):
                    gather(0, c, False, gathered[c])
                with pool.Fori(1, R) as i:
                    for c in range(U):
                        gather(i, c, True, gathered[c])
                pool.sem_inc(S_["wide_merged"], 1)

        @block.scalar
        def _(act):
            act.wait_ge(S_["dve_init"], 2)

            def table_step(s, lo, hi, turn):
                if hi <= NB - 1:
                    n, par = tiles_of(lo), lo % 2
                    act.wait_ge(S_["mv_done"], s + 1)
                    wait(act, "nm_done", s - 1, lo - 1)
                    act.activation(std[:, par, 0:n], mean_var[:, par, 0:n, 1], ACT.Sqrt,
                                   bias=eps_col[:, :]).then_inc(S_["sqrt_done"], 1)
                if lo >= 1 and hi - 1 <= NB - 1:
                    n, par = tiles_of(lo - 1), (lo - 1) % 2
                    act.wait_ge(S_["nm_done"], s)
                    wait(act, "transp_done", s - 2, lo - 2)
                    for t in range(n):
                        tile = (s - 1) * BT + t
                        i = act.activation(h_sb[:, par, t, :], x_sb[:, bass.ds(tile, 1), :].rearrange("p o f -> p (o f)"), ACT.Relu,
                                           bias=neg_mean[:, par, t:t + 1], scale=rstd[:, par, t:t + 1])
                    i.then_inc(S_["relu_done"], 1)
                if lo >= 2 and hi - 2 <= NB - 1:
                    n, par = tiles_of(lo - 2), (lo - 2) % 2
                    act.wait_ge(S_["transp_done"], s - 1)
                    wait(act, "pq_done", s - 3, lo - 3)
                    act.activation(hT_sb[:, par, 0:n, :].rearrange("p t n -> p (t n)"), hT_ps[par][:, 0:n * P],
                                   ACT.Copy).then_inc(S_["hT_done"], 1)
                if lo >= 3 and hi - 3 <= NB - 1:
                    n, par = tiles_of(lo - 3), (lo - 3) % 2
                    act.wait_ge(S_["pq_done"], s - 2)
                    if hi - 3 >= 2:
                        act.wait_ge(S_[f"q_stored{par}"], (turn + (lo - 3) // 2) * 16)
                    act.activation(q_rows[:, par, 0:n, :].rearrange("p t n -> p (t n)"), q_ps[par][:, 0:n * P],
                                   ACT.Copy).then_inc(S_["q_evac"], 1)

            for s in range(T_FIRST):
                table_step(s, s, s, 0)
            with act.Fori(0, (T_BODY - T_FIRST) // 2) as i:
                for c in range(2):
                    table_step(i * 2 + (T_FIRST + c), T_FIRST + c, T_BODY - 2 + c, i)
            for s in range(T_BODY, T_END):
                table_step(s, s, s, 0)

            for half in range(2):
                act.wait_ge(S_["src_T"], half + 1)
                m = 8 * half
                act.activation(src_col[:, :, m:m + 8],
                               col_ps[half][:, 0:8 * R].rearrange("p (m r) -> p r m", m=8), ACT.Copy).then_inc(S_["src_col_ready"], 1)
            act.wait_ge(S_["src_col_ready"], 2)
            act.wait_ge(S_["bias_in"], 48)

            def stage_index(j, c, k):
                r = j // U if isinstance(j, int) else k
                act.activation(idx[:, c, :].rearrange("p (o t) -> p o t", o=1),
                               src_col[:, bass.ds(r, 1), c * GT_:(c + 1) * GT_], ACT.Copy).then_inc(S_["idx_staged"], 1)

            for c in range(U):
                stage_index(c, c, None)

            def group_step(s, lo, hi, turn):
                if hi + U <= NG - 1:
                    c = lo % U
                    act.wait_ge(gathered[c], (turn + 1) * (16 * GT_))
                    stage_index(s + U, c, turn + 1)
                if lo >= 1 and hi - 1 <= NG - 1:
                    act.wait_ge(S_["sum_done"], s)
                    wait(act, "m_done", s - 2, lo - 2)
                    act.activation(H[:, (lo - 1) % 2, :], px_sb[:, (lo - 1) % 2, :], ACT.Relu).then_inc(S_["hidden_done"], 1)
                if hi <= NG - 1:
                    wait(act, "hidden_done", s - 1, lo - 1)
                    act.wait_ge(S_["px_done"], s + 1)
                    act.activation(px_sb[:, lo % 2, :], PX_ps[:, :], ACT.Identity, bias=b1_col[:, :]).then_inc(S_["px_evac"], 1)
                if lo >= 1 and hi - 1 <= NG - 1:
                    act.wait_ge(S_["m_done"], s)
                    wait(act, "scan_done", s - 2, lo - 2)
                    act.activation(M[:, (lo - 1) % 2, :], M_ps[:, :], ACT.Identity, bias=b2_col[:, :]).then_inc(S_["m_evac"], 1)
                if lo >= 2 and hi - 2 <= NG - 1:
                    act.wait_ge(S_["st_done"], s - 1)
                    act.wait_ge(S_["released"], s - 1)
                    act.activation(ST[:, (lo - 2) % U, :, :].rearrange("p t f -> p (t f)"), ST_ps[:, :],
                                   ACT.Copy).then_inc(S_["st_evac"], 1)

            for s in range(U):
                group_step(s, s, s, 0)
            with act.Fori(1, R - 1) as i:
                for c in range(U):
                    group_step(i * U + c, U + c, (R - 2) * U + c, i)
            for s in range(NG - U, G_END):
                group_step(s, s, s, R - 1)

            def fin_copy(b, par, n, again):
                if again:
                    act.wait_ge(S_["fin_T"], b - 1)
                act.activation(outT_block[:, par, 0:n * P], outT[:, bass.ds(b * (BT * P), n * P)],
                               ACT.Copy).then_inc(S_["fin_copied"], 1)

            act.wait_ge(S_["acc_done"], NG)
            fin_copy(0, 0, BT, False)
            fin_copy(1, 1, BT, False)
            with act.Fori(1, (NB - 1) // 2) as i:
                for par in range(2):
                    fin_copy(i * 2 + par, par, BT, True)
            fin_copy(NB - 1, 0, 1, True)

        @block.tensor
        def _(pe):
            pe.wait_ge(S_["ident_ready"], 1)
            pe.wait_ge(S_["wdiff_ready"], 1)

            def columns(rows, half, name):
                for m in range(8):
                    k = 8 * half + m
                    i = pe.transpose(col_ps[half][:, m * R:(m + 1) * R], rows[:, k * P:(k + 1) * P], ident[0:R, 0:R])
                i.then_inc(S_[name], 1)

            pe.wait_ge(S_["src_f_ready"], 1)
            for half in range(2):
                columns(src_row_f, half, "src_T")

            def table_step(s, lo, hi, turn):
                if lo >= 1 and hi - 1 <= NB - 1:
                    n, par = tiles_of(lo - 1), (lo - 1) % 2
                    pe.wait_ge(S_["relu_done"], s)
                    wait(pe, "hT_done", s - 2, lo - 2)
                    for t in range(n):
                        i = pe.transpose(hT_ps[par][:, t * P:(t + 1) * P], h_sb[:, par, t, :], ident[:, :])
                    i.then_inc(S_["transp_done"], 1)
                if lo >= 2 and hi - 2 <= NB - 1:
                    n, par = tiles_of(lo - 2), (lo - 2) % 2
                    pe.wait_ge(S_["hT_done"], s - 1)
                    wait(pe, "q_evac", s - 3, lo - 3)
                    wait(pe, "p_evac", s - 3, lo - 3)
                    for t in range(n):
                        pe.matmul(p_ps[par][:, t * P:(t + 1) * P], hT_sb[:, par, t, :], w1_diff[:, :], start=True, stop=True)
                        i = pe.matmul(q_ps[par][:, t * P:(t + 1) * P], hT_sb[:, par, t, :], w1_sb[:, 1, :], start=True, stop=True)
                    i.then_inc(S_["pq_done"], 1)

            for s in range(T_FIRST):
                table_step(s, s, s, 0)
            with pe.Fori(0, (T_BODY - T_FIRST) // 2) as i:
                for c in range(2):
                    table_step(i * 2 + (T_FIRST + c), T_FIRST + c, T_BODY - 2 + c, i)
            for s in range(T_BODY, T_END):
                table_step(s, s, s, 0)

            pe.wait_ge(S_["rel_last_ready"], 1)
            pe.wait_ge(S_["src_col_ready"], 2)
            for half in range(2):
                columns(rel_last, half, "rel_T")

            def broadcast_rel(c, s, lo):
                pe.matmul(rel_ps[:, :], ones_row[0:1, :], rowbuf[0:1, c, 0, :], start=True, stop=True).then_inc(S_["rel_done"], 1)

            pe.wait_ge(S_["q_evac"], NB)
            pe.wait_ge(S_["p_evac"], NB)
            pe.wait_ge(S_["rel_col_ready"], 2)
            pe.wait_ge(S_["bias_in"], 48)
            pe.wait_ge(row_in[0], 16)
            broadcast_rel(0, 0, 0)

            def group_step(s, lo, hi, turn):
                c = lo % U
                if hi <= NG - 1:
                    pe.wait_ge(gathered[c], (turn + 1) * (16 * GT_))
                    wait(pe, "sum_done", s, lo)
                    for t in range(GT_):
                        i = pe.transpose(GT_ps[:, t * P:(t + 1) * P], G[:, c, t, :], ident[:, :])
                    i.then_inc(S_["gt_done"], 1)
                    pe.wait_ge(win_in[c], (turn + 1) * 16)
                    pe.wait_ge(S_["onehot_done"], s + 1)
                    wait(pe, "px_evac", s, lo)
                    pe.matmul(PX_ps[:, :], p_win[:, c, :], onehot[:, lo % 2, :], start=True, stop=True).then_inc(S_["px_done"], 1)
                if hi + 1 <= NG - 1:
                    nxt = (lo + 1) % U
                    pe.wait_ge(row_in[nxt], (turn + 1 + (1 if nxt == 0 else 0)) * 16)
                    broadcast_rel(nxt, s + 1, lo + 1)
                if lo >= 1 and hi - 1 <= NG - 1:
                    pe.wait_ge(S_["hidden_done"], s)
                    wait(pe, "m_evac", s - 1, lo - 1)
                    pe.matmul(M_ps[:, :], w2_sb[:, :], H[:, (lo - 1) % 2, :], start=True, stop=True).then_inc(S_["m_done"], 1)
                    wait(pe, "scan_done", s - 1, lo - 1)
                    pe.matmul(pen_ps[:, :], ones_row[0:1, :], rowbuf[0:1, (lo - 1) % U, 1, :],
                              start=True, stop=True).then_inc(S_["pen_done"], 1)
                if lo >= 2 and hi - 2 <= NG - 1:
                    pe.wait_ge(S_["scan_done"], s - 1)
                    wait(pe, "st_evac", s - 2, lo - 2)
                    for t in range(GT_):
                        i = pe.transpose(ST_ps[:, t * P:(t + 1) * P], S[:, (lo - 2) % 2, t * P:(t + 1) * P], ident[:, :])
                    i.then_inc(S_["st_done"], 1)
                if lo >= 3 and hi - 3 <= NG - 1:
                    pe.wait_ge(S_["st_evac"], s - 2)
                    pe.wait_ge(S_["L_done"], s - 2)
                    wait(pe, "acc_done", s - 3, lo - 3)
                    for t in range(GT_):
                        i = pe.matmul(sel_ps[:, 0:P], ST[:, (lo - 3) % U, t, :], L[:, (lo - 3) % 2, t, :],
                                      start=(t == 0), stop=(t == GT_ - 1))
                    i.then_inc(S_["sel_done"], 1)

            for s in range(U):
                group_step(s, s, s, 0)
            with pe.Fori(1, R - 1) as i:
                for c in range(U):
                    group_step(i * U + c, U + c, (R - 2) * U + c, i)
            for s in range(NG - U, G_END):
                group_step(s, s, s, R - 1)

            def fin_transpose(b, par, n, again):
                pe.wait_ge(S_["fin_copied"], b + 1)
                if again:
                    pe.wait_ge(S_["fin_added"], b - 1)
                for t in range(n):
                    i = pe.transpose(fin_ps[par][:, t * P:(t + 1) * P], outT_block[:, par, t * P:(t + 1) * P], ident[:, :])
                i.then_inc(S_["fin_T"], 1)

            fin_transpose(0, 0, BT, False)
            fin_transpose(1, 1, BT, False)
            with pe.Fori(1, (NB - 1) // 2) as i:
                for par in range(2):
                    fin_transpose(i * 2 + par, par, BT, True)
            fin_transpose(NB - 1, 0, 1, True)

        @block.vector
        def _(dve):
            dve.memset(src_row[:, :], 0).then_inc(S_["edges_memset"], 1)
            dve.memset(dst_row[:, :, :], NO_NODE).then_inc(S_["edges_memset"], 1)
            dve.memset(dst_next[:, :, :], NO_NODE).then_inc(S_["edges_memset"], 1)
            dve.memset(dst_before[:, :], -1).then_inc(S_["edges_memset"], 1)
            dve.memset(x_sb[:, NT - 1, :], 0.0).then_inc(S_["edges_memset"], 1)
            dve.memset(eps_col[:, :], EPS).then_inc(S_["dve_init"], 1)
            dve.memset(ones_row[:, :], 1.0).then_inc(S_["dve_init"], 1)
            dve.memset(end_row[:, NG - 1:NG], NO_NODE).then_inc(S_["dve_init"], 1)
            dve.wait_ge(S_["pool_init"], 4)
            dve.tensor_copy(iota_part[:, :], iota_part_i[:, :]).then_inc(S_["dve_init"], 1)
            dve.tensor_copy(iota_free1[:, :], iota_free_i[:, :]).then_inc(S_["dve_init"], 1)
            dve.wait_ge(S_["weights_in"], 16)
            dve.tensor_tensor(w1_diff[:, :], w1_sb[:, 0, :], w1_sb[:, 1, :], ALU.subtract).then_inc(S_["wdiff_ready"], 1)
            dve.wait_ge(S_["x_first"], 16)

            def table_step(s, lo, hi, turn):
                if hi <= NB - 1:
                    n, par = tiles_of(lo), lo % 2
                    if lo == hi == X_FIRST:
                        dve.wait_ge(S_["x_rest"], 16)
                    if n == 1:
                        dve.wait_ge(S_["x_tail"], 16)
                    wait(dve, "mv_done", s - 1, lo - 1)
                    for t in range(n):
                        i = dve.bn_stats(stats[:, par, t, :], x_sb[:, bass.ds(s * BT + t, 1), :].rearrange("p o f -> p (o f)"))
                    i.then_inc(S_["stats_done"], 1)
                    wait(dve, "nm_done", s - 1, lo - 1)
                    dve.wait_ge(S_["stats_done"], s + 1)
                    gate(dve)
                    for t in range(n):
                        i = dve.bn_aggr(mean_var[:, par, t, :], stats[:, par, t, :])
                    i.then_inc(S_["mv_done"], 1)
                if lo >= 1 and hi - 1 <= NB - 1:
                    n, par = tiles_of(lo - 1), (lo - 1) % 2
                    dve.wait_ge(S_["sqrt_done"], s)
                    dve.reciprocal(rstd[:, par, 0:n], std[:, par, 0:n]).then_inc(S_["rstd_done"], 1)
                    dve.wait_ge(S_["rstd_done"], s)
                    dve.scalar_tensor_tensor(neg_mean[:, par, 0:n], mean_var[:, par, 0:n, 0], -1.0, rstd[:, par, 0:n],
                                             ALU.mult, ALU.mult).then_inc(S_["nm_done"], 1)
                if lo >= 3 and hi - 3 <= NB - 1:
                    n, par = tiles_of(lo - 3), (lo - 3) % 2
                    dve.wait_ge(S_["pq_done"], s - 2)
                    if hi - 3 >= 2:
                        dve.wait_ge(S_[f"p_stored{par}"], (turn + (lo - 3) // 2) * 16)
                    dve.tensor_copy(p_rows[:, par, 0:n, :].rearrange("p t n -> p (t n)"), p_ps[par][:, 0:n * P]
                                    ).then_inc(S_["p_evac"], 1)

            for s in range(T_FIRST):
                table_step(s, s, s, 0)
            with dve.Fori(0, (T_BODY - T_FIRST) // 2) as i:
                for c in range(2):
                    table_step(i * 2 + (T_FIRST + c), T_FIRST + c, T_BODY - 2 + c, i)
            for s in range(T_BODY, T_END):
                table_step(s, s, s, 0)

            dve.wait_ge(S_["base_in"], 32)
            dve.wait_ge(S_["dve_init"], 5)
            dve.tensor_tensor(wide_row[:, :], end_row[:, :], base_row[:, :], ALU.subtract).then_inc(S_["dve_small"], 1)
            dve.wait_ge(S_["dve_small"], 1)
            dve.tensor_scalar(end_row[:, :], wide_row[:, :], float(P) - 0.5, None, ALU.is_ge).then_inc(S_["dve_small"], 1)
            dve.wait_ge(S_["dve_small"], 2)
            dve.reduce_max(any_wide_i[:, :], end_row[:, :], AX.X).then_inc(S_["anyw_ready"], 1)
            dve.wait_ge(S_["rel_i_ready"], 1)
            dve.tensor_scalar(wide[:, :], rel_i[:, :, GE - 1], float(P) - 0.5, None, ALU.is_ge).then_inc(S_["wide_ready"], 1)
            dve.wait_ge(S_["wide_ready"], 1)
            dve.tensor_scalar(wide_off[:, :], wide[:, :], WIDE_OFF, None, ALU.mult).then_inc(S_["woff_ready"], 1)
            dve.wait_ge(S_["woff_ready"], 1)
            dve.tensor_tensor(rowpack[:, :, 0, :], rel_i[:, :, :],
                              wide_off[:, :].rearrange("r (u o) -> r u o", o=1).to_broadcast([R, U, GE]),
                              ALU.add).then_inc(S_["rel_row_ready"], 1)
            dve.wait_ge(S_["dst_in"], 32)
            dve.wait_ge(S_["dstn_in"], 32)
            dve.tensor_tensor(last[:, :].rearrange("r (u e) -> r u e", u=U), dst_row[:, :, :], dst_next[:, :, :],
                              ALU.not_equal).then_inc(S_["last_ready"], 1)
            dve.wait_ge(S_["before_in"], 16)
            dve.tensor_tensor(start[:, 0:1], dst_row[:, 0, 0:1], dst_before[:, :], ALU.not_equal).then_inc(S_["start_ready"], 1)
            dve.wait_ge(S_["last_ready"], 1)
            dve.tensor_scalar(rowpack[:, 0, 1, 1:GE], last[:, 0:GE - 1], PENALTY, None, ALU.mult)
            dve.tensor_scalar(rowpack[:, 1:U, 1, :], last[:, GE - 1:RE - 1].rearrange("r (u e) -> r u e", u=U - 1),
                              PENALTY, None, ALU.mult)
            dve.wait_ge(S_["start_ready"], 1)
            dve.tensor_scalar(rowpack[:, 0, 1, 0:1], start[:, 0:1], PENALTY, None, ALU.mult).then_inc(S_["pen_ready"], 1)
            dve.wait_ge(S_["rel_row_ready"], 1)
            dve.scalar_tensor_tensor(rel_last[:, :].rearrange("r (u e) -> r u e", u=U), rowpack[:, :, 0, :], 1.0,
                                     last[:, :].rearrange("r (u e) -> r u e", u=U), ALU.add, ALU.mult
                                     ).then_inc(S_["rel_last_ready"], 1)
            for half in range(2):
                dve.wait_ge(S_["rel_T"], half + 1)
                dve.tensor_copy(rel_last_col[:, :, 8 * half:8 * half + 8],
                                col_ps[half][:, 0:8 * R].rearrange("p (m r) -> p r m", m=8)).then_inc(S_["rel_col_ready"], 1)
            dve.wait_ge(S_["rel_col_ready"], 2)
            dve.wait_ge(S_["outT_zero"], 1)

            def one_hot(s, lo):
                dve.wait_ge(S_["rel_done"], s + 1)
                wait(dve, "px_done", s - 1, lo - 1)
                dve.tensor_scalar(onehot[:, lo % 2, :], rel_ps[:, :], iota_part[:, 0:1], None,
                                  ALU.is_equal).then_inc(S_["onehot_done"], 1)

            one_hot(0, 0)

            def group_step(s, lo, hi, turn):
                if hi <= NG - 1:
                    dve.wait_ge(S_["gt_done"], s + 1)
                    dve.wait_ge(S_["px_evac"], s + 1)
                    dve.tensor_tensor(px_sb[:, lo % 2, :], GT_ps[:, :], px_sb[:, lo % 2, :], ALU.add
                                      ).then_inc(S_["sum_done"], 1)
                if hi + 1 <= NG - 1:
                    one_hot(s + 1, lo + 1)
                if lo >= 1 and hi - 1 <= NG - 1:
                    dve.wait_ge(S_["m_evac"], s)
                    dve.wait_ge(S_["pen_done"], s)
                    wait(dve, "st_done", s - 2, lo - 2)
                    wait(dve, "scan_done", s - 1, lo - 1)
                    k = (lo - 1) % 2
                    initial = 0.0 if lo == 1 else S[:, 1 - k, GE - 1:GE]
                    dve.tensor_tensor_scan(S[:, k, :], pen_ps[:, :], M[:, k, :], initial, ALU.add, ALU.max
                                           ).then_inc(S_["scan_done"], 1)
                if lo >= 2 and hi - 2 <= NG - 1:
                    wait(dve, "sel_done", s - 3, lo - 3)
                    row = (lo - 2) // U if lo == hi else (turn - 1 if lo % U < 2 else turn)
                    for t in range(GT_):
                        m = ((lo - 2) % U) * GT_ + t
                        i = dve.tensor_scalar(L[:, (lo - 2) % 2, t, :], iota_free1[:, :],
                                              rel_last_col[:, bass.ds(row, 1), m:m + 1].rearrange("p o t -> p (o t)"),
                                              None, ALU.is_equal)
                    i.then_inc(S_["L_done"], 1)
                if lo >= 3 and hi - 3 <= NG - 1:
                    base = dve.value_load(base_row[0:1, bass.ds(s - 3, 1)], min_val=0, max_val=N - 1)
                    dve.wait_ge(S_["sel_done"], s - 2)
                    wait(dve, "acc_done", s - 3, lo - 3)
                    dve.tensor_tensor(outT[:, bass.ds(base, P)], outT[:, bass.ds(base, P)], sel_ps[:, 0:P],
                                      ALU.add).then_inc(S_["acc_done"], 1)

            for s in range(U):
                group_step(s, s, s, 0)
            with dve.Fori(1, R - 1) as i:
                for c in range(U):
                    group_step(i * U + c, U + c, (R - 2) * U + c, i)
            for s in range(NG - U, G_END):
                group_step(s, s, s, R - 1)

            dve.wait_ge(S_["wide_merged"], 1)

            def fin_add(b, par, n):
                dve.wait_ge(S_["fin_T"], b + 1)
                tiles = x_sb[:, bass.ds(b * BT, n), :].rearrange("p t f -> p (t f)")
                dve.tensor_tensor(tiles, tiles, fin_ps[par][:, 0:n * P], ALU.add).then_inc(S_["fin_added"], 1)

            with dve.Fori(0, (NB - 1) // 2) as i:
                for par in range(2):
                    fin_add(i * 2 + par, par, BT)
            fin_add(NB - 1, 0, 1)


_INS = ['x', 'src', 'dst', 'L0_gnn_W1', 'L0_gnn_b1', 'L0_gnn_W2', 'L0_gnn_b2']


def kernel(**inputs):
    import numpy as _np
    import concourse.bacc as _bacc
    from concourse import mybir as _mybir
    from concourse.bass_utils import run_bass_kernel_spmd as _run

    nc = _bacc.Bacc("TRN2", target_bir_lowering=False, num_devices=1)
    arrays, args = {}, []
    for name in _INS:
        a = _np.ascontiguousarray(inputs[name])
        arrays[f"in_{name}_dram"] = a
        args.append(nc.dram_tensor(f"in_{name}_dram", a.shape, _mybir.dt.from_np(a.dtype), kind="ExternalInput").ap())
    shape = inputs["x"].shape
    args.append(nc.dram_tensor("out_0_dram", shape, _mybir.dt.float32, kind="ExternalOutput").ap())
    gnn_kernel(nc, *args)
    r = _run(nc, [arrays], core_ids=[0])
    return r.results[0]["out_0_dram"]
```

```python
from contextlib import ExitStack

import concourse.bass as bass
from concourse import mybir


def gnn_kernel(nc, x, src, dst, w1, b1, w2, b2, out):
    f32, bf16, i32 = mybir.dt.float32, mybir.dt.bfloat16, mybir.dt.int32
    ALU, ACT, AX = mybir.AluOpType, mybir.ActivationFunctionType, mybir.AxisListType

    N, F = x.shape
    E = src.shape[0]
    P = 128
    GE = 512
    WN = 64
    GT_ = GE // P
    U = 4
    RE = U * GE
    R = -(-E // RE)
    NG = R * U
    E_FULL = (R - 1) * RE
    E_TAIL = E - E_FULL
    NT = -(-N // P)
    N_FULL = (NT - 1) * P
    N_TAIL = N - N_FULL
    BT = 4
    NB = -(-NT // BT)
    LAST_TILES = -(-(E - (NG - 1) * GE) // P)
    assert 0 < LAST_TILES <= GT_
    assert NT == (NB - 1) * BT + 1 and (NB - 1) % 2 == 0 and 0 < E_TAIL < RE and N_TAIL > 0
    NPAD = (NT + 1) * P
    NO_NODE = N
    WIDE_OFF = 1024.0
    NO_SCATTER = 20000.0
    PENALTY = -3.0e38
    EPS = 1e-5
    LAG = 4

    q_table = nc.dram_tensor("q_table", (N, F), f32, kind="Internal").ap()
    p_table = nc.dram_tensor("p_table", (NPAD, F), f32, kind="Internal").ap()
    rows_dram = nc.dram_tensor("rows_dram", (R, U * 2 * GE), bf16, kind="Internal").ap()
    p_index = nc.dram_tensor("p_index", (R, RE), i32, kind="Internal").ap()
    s_index = nc.dram_tensor("s_index", (R, RE), i32, kind="Internal").ap()
    wide_out = nc.dram_tensor("wide_out", (NT * P, F), f32, kind="Internal").ap()

    ctx = ExitStack()
    with ctx:
        def sb(name, shape, dt):
            return ctx.enter_context(nc.sbuf_tensor(name, shape, dt))

        def sem(name):
            return ctx.enter_context(nc.semaphore(name))

        ident = sb("ident", [P, P], f32)
        ones = sb("ones", [P, P], bf16)
        iota_part_i = sb("iota_part_i", [P, 1], i32)
        iota_part = sb("iota_part", [P, 1], f32)
        iota_free_i = sb("iota_free_i", [P, P], i32)
        iota_free1 = sb("iota_free1", [P, P], f32)
        eps_col = sb("eps_col", [P, 1], f32)
        w1_sb = sb("w1_sb", [P, 2, F], f32)
        w1_diff = sb("w1_diff", [P, F], f32)
        w2_sb = sb("w2_sb", [P, F], f32)
        b1_col = sb("b1_col", [P, 1], f32)
        b2_col = sb("b2_col", [P, 1], f32)
        zeros = sb("zeros", [P, F], f32)
        x_sb = sb("x_sb", [P, NT, F], f32)
        stats = sb("stats", [P, 2, BT, 6], f32)
        mean_var = sb("mean_var", [P, 2, BT, 2], f32)
        std = sb("std", [P, 2, BT], f32)
        rstd = sb("rstd", [P, 2, BT], f32)
        neg_mean = sb("neg_mean", [P, 2, BT], f32)
        h_sb = sb("h_sb", [P, 2, BT, F], f32)
        hT_sb = sb("hT_sb", [P, 2, BT, P], f32)
        p_rows = sb("p_rows", [P, 2, BT, F], f32)
        q_rows = sb("q_rows", [P, 2, BT, F], f32)
        outT = sb("outT", [P, NPAD], f32)
        outT_block = sb("outT_block", [P, 2, BT * P], f32)
        src_row = sb("src_row", [R, RE], i32)
        src_row_f = sb("src_row_f", [R, RE], f32)
        dst_row = sb("dst_row", [R, U, GE], i32)
        dst_next = sb("dst_next", [R, U, GE], i32)
        dst_before = sb("dst_before", [R, 1], i32)
        rel_i = sb("rel_i", [R, U, GE], i32)
        last = sb("last", [R, RE], f32)
        wide = sb("wide", [R, U], f32)
        wide_off = sb("wide_off", [R, U], f32)
        rel_last = sb("rel_last", [R, RE], f32)
        start = sb("start", [R, RE], f32)
        rowpack = sb("rowpack", [R, U, 2, GE], bf16)
        base_row = sb("base_row", [1, NG], i32)
        end_row = sb("end_row", [1, NG], i32)
        wide_row = sb("wide_row", [1, NG], f32)
        any_wide_i = sb("any_wide_i", [1, 1], i32)
        src_col = sb("src_col", [P, R, U * GT_], i32)
        rel_last_col = sb("rel_last_col", [P, R, U * GT_], f32)
        idx = sb("idx", [P, U, GT_], i32)
        G = sb("G", [P, U, GT_, F], f32)
        p_win = sb("p_win", [P, U, F], f32)
        rowbuf = sb("rowbuf", [P, U, 2, GE], bf16)
        onehot = sb("onehot", [P, 2, GE], f32)
        px_sb = sb("px_sb", [P, 2, GE], f32)
        H = sb("H", [P, 2, GE], f32)
        M = sb("M", [P, 2, GE], f32)
        S = sb("S", [P, 2, GE], f32)
        L = sb("L", [P, 2, GT_, WN], f32)
        ST = sb("ST", [P, U, GT_, F], f32)
        idx_p = sb("idx_p", [P, U, GT_], i32)
        idx_s = sb("idx_s", [P, U, GT_], i32)

        bank = [ctx.enter_context(nc.psum_tensor(f"bank{i}", [P, GE], f32)) for i in range(8)]
        hT_ps, p_ps, q_ps = bank[0:2], bank[2:4], bank[4:6]
        col_ps = bank[6:8]
        GT_ps, PX_ps, rel_ps, pen_ps, M_ps, ST_ps, sel_ps = bank[0:7]
        fin_ps = bank[0:2]

        S_ = {n: sem(n) for n in """
            loop_zeroed h_pool h_scaled dve_init pool_init ident_ready weights_in wdiff_ready
            src_in dst_in dstn_in before_in before_main edges_memset base_in bias_in
            x_block x_first x_rest x_tail
            stats_done mv_done sqrt_done rstd_done nm_done h_act transp_done hT_done pq_done q_evac p_evac
            q_stored0 q_stored1 p_stored0 p_stored1 p_zero
            src_f_ready src_T src_col_ready rel_i_ready last_ready wide_ready woff_ready
            rel_row_ready rel_last_ready start_ready pen_ready rel_T rel_col_ready rows_stored anyw_ready dve_small
            idx_staged rel_done onehot_done gt_done px_done px_evac gates sum_done hidden_done m_done m_evac
            pen_done scan_done st_done st_evac L_done sel_done acc_done
            released wide_merged fin_copied fin_T fin_added out_stored outT_zero
            slow_v slow_store slow_idx slow_gather slow_scatter slow_zero
            """.split()}
        gathered = [sem(f"gathered{c}") for c in range(U)]
        win_in = [sem(f"win_in{c}") for c in range(U)]
        row_in = [sem(f"row_in{c}") for c in range(U)]

        def wait(eng, name, value, least):
            if least > 0:
                eng.wait_ge(S_[name] if isinstance(name, str) else name, value)

        def gate(eng):
            eng.sem_inc(S_["gates"], 1)

        T_FIRST, T_BODY, T_END = 6, NB - 1, NB + 4
        PA = 2
        X_FIRST = 5
        G_FIRST, G_BODY, G_END = U, NG, NG + 3

        def tiles_of(least):
            return 1 if least == NB - 1 else BT

        block = ctx.enter_context(nc.Block())

        @block.sync
        def _(sp):
            src_full = src[0:E_FULL].rearrange("(r e) -> r e", e=RE)
            src_tail = src[E_FULL:E].rearrange("(r e) -> r e", r=1)
            tiles = x[0:N_FULL, :].rearrange("(t p) f -> p t f", p=P)
            third = X_FIRST * BT
            sp.dma_start(x_sb[:, 0:BT, :], tiles[:, 0:BT, :]).then_inc(S_["x_block"], 16)
            sp.wait_ge(S_["edges_memset"], 5)
            sp.dma_start(src_row[0:R - 1, :], src_full).then_inc(S_["src_in"], 16)
            sp.dma_start(src_row[R - 1:R, 0:E_TAIL], src_tail).then_inc(S_["src_in"], 16)
            sp.dma_start(x_sb[:, BT:third, :], tiles[:, BT:third, :]).then_inc(S_["x_first"], 16)
            sp.dma_start(w1_sb[:, :, :], w1.rearrange("(a k) f -> k a f", a=2)).then_inc(S_["weights_in"], 16)
            sp.dma_start(x_sb[:, third:NT - 1, :], tiles[:, third:NT - 1, :]).then_inc(S_["x_rest"], 16)
            sp.dma_start(x_sb[0:N_TAIL, NT - 1, :], x[N_FULL:N, :]).then_inc(S_["x_tail"], 16)
            dst_full = dst[0:E_FULL].rearrange("(r e) -> r e", e=RE)
            dst_tail = dst[E_FULL:E].rearrange("(r e) -> r e", r=1)
            dst_flat = dst_row[:, :, :].rearrange("r u e -> r (u e)")
            sp.dma_start(dst_flat[0:R - 1, :], dst_full).then_inc(S_["dst_in"], 16)
            sp.dma_start(dst_flat[R - 1:R, 0:E_TAIL], dst_tail).then_inc(S_["dst_in"], 16)
            next_flat = dst_next[:, :, :].rearrange("r u e -> r (u e)")
            sp.dma_start(next_flat[0:R - 1, :], dst[1:E_FULL + 1].rearrange("(r e) -> r e", e=RE)).then_inc(S_["dstn_in"], 16)
            sp.dma_start(next_flat[R - 1:R, 0:E_TAIL - 1],
                         dst[E_FULL + 1:E].rearrange("(r e) -> r e", r=1)).then_inc(S_["dstn_in"], 16)
            sp.dma_start(w2_sb[:, :], w2).then_inc(S_["bias_in"], 16)
            sp.dma_start(b1_col[:, :], b1.rearrange("(k a) -> k a", a=1)).then_inc(S_["bias_in"], 16)
            sp.dma_start(b2_col[:, :], b2.rearrange("(k a) -> k a", a=1)).then_inc(S_["bias_in"], 16)
            with nc.allow_non_contiguous_dma(reason="one number of each group or row"):
                sp.dma_start(dst_before[1:R, :], bass.AP(dst.tensor, RE - 1, [[RE, R - 1], [1, 1]])).then_inc(S_["before_in"], 16)
                sp.dma_start(base_row[:, :], bass.AP(dst.tensor, 0, [[GE * NG, 1], [GE, NG]])).then_inc(S_["base_in"], 16)
                sp.dma_start(end_row[:, 0:NG - 1], bass.AP(dst.tensor, GE - 1, [[GE * NG, 1], [GE, NG - 1]])).then_inc(S_["base_in"], 16)
            sp.wait_ge(S_["pool_init"], 1)
            sp.dma_start(p_table[N:N_FULL + P, :], zeros[0:P - N_TAIL, :]).then_inc(S_["p_zero"], 16)
            sp.dma_start(p_table[N_FULL + P:NPAD, :], zeros[:, :]).then_inc(S_["p_zero"], 16)

            def store_tables(b, par):
                rows = (b * BT) * P if isinstance(b, int) else b * (BT * P)
                sp.wait_ge(S_["q_evac"], b + 1)
                sp.dma_start(q_table[bass.ds(rows, BT * P), :].rearrange("(t p) f -> p t f", p=P),
                             q_rows[:, par, :, :]).then_inc(S_[f"q_stored{par}"], 16)
                sp.wait_ge(S_["p_evac"], b + 1)
                sp.dma_start(p_table[bass.ds(rows, BT * P), :].rearrange("(t p) f -> p t f", p=P),
                             p_rows[:, par, :, :]).then_inc(S_[f"p_stored{par}"], 16)

            with sp.Fori(0, (NB - 1) // 2) as i:
                for par in range(2):
                    store_tables(i * 2 + par, par)
            sp.wait_ge(S_["q_evac"], NB)
            sp.dma_start(q_table[N_FULL:N, :], q_rows[0:N_TAIL, 0, 0, :]).then_inc(S_["q_stored0"], 16)
            sp.wait_ge(S_["p_evac"], NB)
            sp.dma_start(p_table[N_FULL:N, :], p_rows[0:N_TAIL, 0, 0, :]).then_inc(S_["p_stored0"], 16)

            sp.wait_ge(S_["rel_row_ready"], 1)
            sp.wait_ge(S_["pen_ready"], 1)
            sp.dma_start(rows_dram[:, :], rowpack[:, :, :, :].rearrange("r u a e -> r (u a e)")).then_inc(S_["rows_stored"], 16)
            sp.wait_ge(S_["p_zero"], 32)
            sp.wait_ge(S_["p_stored0"], 16 * ((NB - 1) // 2 + 1))
            sp.wait_ge(S_["p_stored1"], 16 * ((NB - 1) // 2))
            sp.wait_ge(S_["base_in"], 32)
            sp.wait_ge(S_["rows_stored"], 16)
            sp.wait_ge(S_["loop_zeroed"], 2)
            rows_by_turn = rows_dram.rearrange("r (u c) -> r u c", u=U)

            def load_group(i, c, again):
                j = i * U + c
                if again:
                    sp.wait_ge(S_["px_done"], i * U + (c - U + 1))
                base = sp.value_load(base_row[0:1, bass.ds(j, 1)], min_val=0, max_val=N - 1)
                sp.dma_start(p_win[0:WN, c, :], p_table[bass.ds(base, WN), :]).then_inc(win_in[c], 16)
                if again:
                    sp.wait_ge(S_["pen_done"], i * U + (c - U + 1))
                sp.dma_start(rowbuf[0:1, c, :, :].rearrange("o a e -> o (a e)"),
                             rows_by_turn[bass.ds(i, 1), c, :]).then_inc(row_in[c], 16)

            for c in range(U):
                load_group(0, c, False)
            with sp.Fori(1, R) as i:
                for c in range(U):
                    load_group(i, c, True)

            out_tiles = out[0:N_FULL, :].rearrange("(t p) f -> p t f", p=P)
            with sp.Fori(0, (NB - 1) // 2) as b:
                sp.wait_ge(S_["fin_added"], b * 2 + 2)
                sp.dma_start(out[bass.ds(b * (2 * BT * P), 2 * BT * P), :].rearrange("(t p) f -> p t f", p=P),
                             x_sb[:, bass.ds(b * (2 * BT), 2 * BT), :]).then_inc(S_["out_stored"], 16)
            sp.wait_ge(S_["fin_added"], NB)
            sp.dma_start(out[N_FULL:N, :], x_sb[0:N_TAIL, NT - 1, :]).then_inc(S_["out_stored"], 16)
            sp.wait_ge(S_["out_stored"], 16 * ((NB - 1) // 2 + 1))

        @block.gpsimd
        def _(pool):
            pool.memset(zeros[:, :], 0.0).then_inc(S_["pool_init"], 1)
            pool.memset(ident[:, :], 0.0).then_inc(S_["pool_init"], 1)
            pool.iota(iota_part_i[:, :], pattern=[[0, 1]], base=0, channel_multiplier=1).then_inc(S_["pool_init"], 1)
            pool.iota(iota_free_i[:, :], pattern=[[1, P]], base=1, channel_multiplier=0).then_inc(S_["pool_init"], 1)
            pool.wait_ge(S_["pool_init"], 2)
            pool.affine_select(out=ident[:, :], in_=ident[:, :], compare_op=ALU.not_equal, fill=1.0, base=0,
                               pattern=[[-1, P]], channel_multiplier=1).then_inc(S_["ident_ready"], 1)
            pool.memset(rowbuf[:, :, :, :], 0.0).then_inc(S_["loop_zeroed"], 1)

            def normalise(s, par, turn):
                n = BT - PA
                h = h_sb[:, par, PA:BT, :]
                spread = lambda t: t[:, par, PA:BT].rearrange("p (t o) -> p t o", o=1).to_broadcast([P, n, F])
                pool.wait_ge(S_["nm_done"], s + 1)
                if par + 2 * turn >= 2 if isinstance(turn, int) else True:
                    pool.wait_ge(S_["transp_done"], s - 1)
                gate(pool)
                pool.tensor_tensor(h, x_sb[:, bass.ds(s * BT + PA, n), :], spread(rstd), ALU.mult).then_inc(S_["h_scaled"], 1)
                pool.wait_ge(S_["h_scaled"], s + 1)
                gate(pool)
                pool.tensor_tensor(h, h, spread(neg_mean), ALU.add).then_inc(S_["h_pool"], 1)

            for par in range(2):
                normalise(par, par, 0)
            with pool.Fori(1, (NB - 1) // 2) as i:
                for par in range(2):
                    normalise(i * 2 + par, par, i)
            pool.wait_ge(S_["dst_in"], 32)
            pool.tensor_tensor(rel_i[:, :, :], dst_row[:, :, :], dst_row[:, :, 0:1].to_broadcast([R, U, GE]),
                               ALU.subtract).then_inc(S_["rel_i_ready"], 1)
            pool.wait_ge(S_["anyw_ready"], 1)
            any_wide = pool.value_load(any_wide_i[0:1, 0:1], min_val=0, max_val=1)
            pool.wait_ge(S_["q_stored0"], 16 * ((NB - 1) // 2 + 1))
            pool.wait_ge(S_["q_stored1"], 16 * ((NB - 1) // 2))

            def gather(i, c, again, signal, tiles=GT_):
                pool.wait_ge(S_["idx_staged"], i * U + (c + 1))
                if again:
                    pool.wait_ge(S_["gt_done"], i * U + (c - U + 1))
                gate(pool)
                for t in range(tiles):
                    pool.indirect_dma_start(G[:, c, t, :], None, q_table[:, :],
                                            bass.IndirectOffsetOnAxis(ap=idx[:, c, t:t + 1], axis=0)).then_inc(signal, 16)

            def slow_setup():
                v = [0]

                def chain(instruction):
                    v[0] += 1
                    instruction.then_inc(S_["slow_v"], 1)
                    pool.wait_ge(S_["slow_v"], v[0])

                pool.dma_start(wide_out.rearrange("(t p) f -> p t f", p=P),
                               zeros[:, :].rearrange("p (a f) -> p a f", a=1).to_broadcast([P, NT, F])).then_inc(S_["slow_zero"], 16)
                pool.wait_ge(S_["src_T"], 2)
                pool.wait_ge(S_["wide_ready"], 1)
                d, a = src_row_f, src_row
                by_group = lambda t: t[:, :].rearrange("r (u e) -> r u e", u=U)
                spread = wide[:, :].rearrange("r (u o) -> r u o", o=1).to_broadcast([R, U, GE])
                chain(pool.tensor_copy(d[:, :], dst_row[:, :, :].rearrange("r u e -> r (u e)")))
                chain(pool.tensor_scalar(d[:, :], d[:, :], -float(NO_NODE), None, ALU.add))
                chain(pool.tensor_tensor(by_group(d), by_group(d), spread, ALU.mult))
                chain(pool.tensor_scalar(a[:, :], d[:, :], float(NO_NODE), None, ALU.add))
                pool.dma_start(p_index[:, :], a[:, :]).then_inc(S_["slow_store"], 16)
                pool.wait_ge(S_["slow_store"], 16)
                chain(pool.tensor_copy(d[:, :], dst_row[:, :, :].rearrange("r u e -> r (u e)")))
                chain(pool.tensor_scalar(d[:, :], d[:, :], -NO_SCATTER, None, ALU.add))
                chain(pool.tensor_tensor(by_group(d), by_group(d), spread, ALU.mult))
                pool.wait_ge(S_["last_ready"], 1)
                chain(pool.tensor_tensor(d[:, :], d[:, :], last[:, :], ALU.mult))
                chain(pool.tensor_scalar(a[:, :], d[:, :], NO_SCATTER, None, ALU.add))
                pool.dma_start(s_index[:, :], a[:, :]).then_inc(S_["slow_store"], 16)
                pool.wait_ge(S_["slow_store"], 32)
                pool.wait_ge(S_["slow_zero"], 16)
                pool.wait_ge(S_["p_zero"], 32)
                pool.wait_ge(S_["p_stored0"], 16 * ((NB - 1) // 2 + 1))
                pool.wait_ge(S_["p_stored1"], 16 * ((NB - 1) // 2))

            p_cols = p_index.rearrange("r (u t p) -> p (r u) t", p=P, t=GT_)
            s_cols = s_index.rearrange("r (u t p) -> p (r u) t", p=P, t=GT_)

            def slow_gather(i, c, again, tiles=GT_):
                j = i * U + c
                if again:
                    pool.wait_ge(S_["slow_scatter"], (j - (U - 1)) * (16 * GT_))
                with nc.allow_non_contiguous_dma(reason="an index per partition"):
                    gate(pool)
                    pool.dma_start(idx_p[:, c, :].rearrange("p (o t) -> p o t", o=1),
                                   p_cols[:, bass.ds(j, 1), :]).then_inc(S_["slow_idx"], 16)
                    pool.wait_ge(S_["slow_idx"], (j * 2 + 1) * 16)
                    gate(pool)
                    pool.dma_start(idx_s[:, c, :].rearrange("p (o t) -> p o t", o=1),
                                   s_cols[:, bass.ds(j, 1), :]).then_inc(S_["slow_idx"], 16)
                    pool.wait_ge(S_["slow_idx"], (j * 2 + 2) * 16)
                gather(i, c, again, S_["slow_gather"], tiles)
                pool.wait_ge(S_["slow_gather"], (j + 1) * (16 * GT_) - 16 * (GT_ - tiles))
                gate(pool)
                for t in range(tiles):
                    pool.indirect_dma_start(G[:, c, t, :], None, p_table[:, :],
                                            bass.IndirectOffsetOnAxis(ap=idx_p[:, c, t:t + 1], axis=0),
                                            compute_op=ALU.add).then_inc(gathered[c], 16)

            def slow_scatter(i, c):
                j = i * U + c
                pool.wait_ge(S_["st_evac"], j + 1)
                gate(pool)
                for t in range(GT_):
                    pool.indirect_dma_start(wide_out[:, :], bass.IndirectOffsetOnAxis(ap=idx_s[:, c, t:t + 1], axis=0),
                                            ST[:, c, t, :], None, bounds_check=N - 1, oob_is_err=False
                                            ).then_inc(S_["slow_scatter"], 16)
                pool.wait_ge(S_["slow_scatter"], (j + 1) * (16 * GT_))
                pool.sem_inc(S_["released"], 1)

            pool.sem_inc(S_["released"], U)
            with pool.If(any_wide > 0):
                slow_setup()
                for c in range(U):
                    slow_gather(0, c, False)
                with pool.Fori(1, R - 1) as i:
                    for c in range(U):
                        slow_scatter(i - 1, c)
                        slow_gather(i, c, True)
                for c in range(U):
                    slow_scatter(R - 2, c)
                    slow_gather(R - 1, c, True, GT_ if c < U - 1 else LAST_TILES)
                for c in range(U):
                    slow_scatter(R - 1, c)
                pool.dma_start(x_sb[:, :, :], wide_out.rearrange("(t p) f -> p t f", p=P),
                               accum_op=ALU.add).then_inc(S_["slow_zero"], 16)
                pool.wait_ge(S_["slow_zero"], 32)
                pool.sem_inc(S_["wide_merged"], 1)
            with pool.Else():
                pool.sem_inc(S_["released"], NG)
                for c in range(U):
                    gather(0, c, False, gathered[c])
                with pool.Fori(1, R - 1) as i:
                    for c in range(U):
                        gather(i, c, True, gathered[c])
                for c in range(U):
                    gather(R - 1, c, True, gathered[c], GT_ if c < U - 1 else LAST_TILES)
                pool.sem_inc(S_["wide_merged"], 1)

        @block.scalar
        def _(act):
            act.wait_ge(S_["src_in"], 32)
            act.activation(src_row_f[:, :], src_row[:, :], ACT.Copy).then_inc(S_["src_f_ready"], 1)
            for half in range(2):
                act.wait_ge(S_["src_T"], half + 1)
                m = 8 * half
                act.activation(src_col[:, :, m:m + 8],
                               col_ps[half][:, 0:8 * R].rearrange("p (m r) -> p r m", m=8),
                               ACT.Copy).then_inc(S_["src_col_ready"], 1)
            act.wait_ge(S_["dve_init"], 2)

            def table_step(s, lo, hi, turn):
                if lo >= 3 and hi - 3 <= NB - 1:
                    n, par = tiles_of(lo - 3), (lo - 3) % 2
                    act.wait_ge(S_["transp_done"], s - 2)
                    wait(act, "pq_done", s - 4, lo - 4)
                    act.activation(hT_sb[:, par, 0:n, :].rearrange("p t n -> p (t n)"), hT_ps[par][:, 0:n * P],
                                   ACT.Relu).then_inc(S_["hT_done"], 1)
                if lo >= 1 and hi - 1 <= NB - 1:
                    n, par = min(PA, tiles_of(lo - 1)), (lo - 1) % 2
                    act.wait_ge(S_["nm_done"], s)
                    wait(act, "transp_done", s - 2, lo - 2)
                    for t in range(n):
                        tile = (s - 1) * BT + t
                        i = act.activation(h_sb[:, par, t, :], x_sb[:, bass.ds(tile, 1), :].rearrange("p o f -> p (o f)"), ACT.Identity,
                                           bias=neg_mean[:, par, t:t + 1], scale=rstd[:, par, t:t + 1])
                    i.then_inc(S_["h_act"], 1)
                if hi <= NB - 1:
                    n, par = tiles_of(lo), lo % 2
                    act.wait_ge(S_["mv_done"], s + 1)
                    wait(act, "nm_done", s - 1, lo - 1)
                    act.activation(std[:, par, 0:n], mean_var[:, par, 0:n, 1], ACT.Sqrt,
                                   bias=eps_col[:, :]).then_inc(S_["sqrt_done"], 1)
                if lo >= 4 and hi - 4 <= NB - 1:
                    n, par = tiles_of(lo - 4), (lo - 4) % 2
                    act.wait_ge(S_["pq_done"], s - 3)
                    if hi - 4 >= 2:
                        act.wait_ge(S_[f"q_stored{par}"], (turn + (lo - 4) // 2) * 16)
                    act.activation(q_rows[:, par, 0:n, :].rearrange("p t n -> p (t n)"), q_ps[par][:, 0:n * P],
                                   ACT.Copy).then_inc(S_["q_evac"], 1)

            for s in range(T_FIRST):
                table_step(s, s, s, 0)
            with act.Fori(0, (T_BODY - T_FIRST) // 2) as i:
                for c in range(2):
                    table_step(i * 2 + (T_FIRST + c), T_FIRST + c, T_BODY - 2 + c, i)
            for s in range(T_BODY, T_END):
                table_step(s, s, s, 0)
            act.wait_ge(S_["src_col_ready"], 2)
            act.wait_ge(S_["bias_in"], 48)

            def stage_index(j, c, k):
                r = j // U if isinstance(j, int) else k
                act.activation(idx[:, c, :].rearrange("p (o t) -> p o t", o=1),
                               src_col[:, bass.ds(r, 1), c * GT_:(c + 1) * GT_], ACT.Copy).then_inc(S_["idx_staged"], 1)

            for c in range(U):
                stage_index(c, c, None)
            act.activation(outT[:, :].rearrange("p (t f) -> p t f", f=F),
                           zeros[:, :].rearrange("p (a f) -> p a f", a=1).to_broadcast([P, NPAD // F, F]),
                           ACT.Copy).then_inc(S_["outT_zero"], 1)

            def group_step(s, lo, hi, turn):
                if hi + U <= NG - 1:
                    c = lo % U
                    act.wait_ge(gathered[c], (turn + 1) * (16 * GT_))
                    stage_index(s + U, c, turn + 1)
                if lo >= 1 and hi - 1 <= NG - 1:
                    act.wait_ge(S_["sum_done"], s)
                    wait(act, "m_done", s - 2, lo - 2)
                    act.activation(H[:, (lo - 1) % 2, :], px_sb[:, (lo - 1) % 2, :], ACT.Relu).then_inc(S_["hidden_done"], 1)
                if hi <= NG - 1:
                    wait(act, "hidden_done", s - 1, lo - 1)
                    act.wait_ge(S_["px_done"], s + 1)
                    act.activation(px_sb[:, lo % 2, :], PX_ps[:, :], ACT.Identity, bias=b1_col[:, :]).then_inc(S_["px_evac"], 1)
                if lo >= 1 and hi - 1 <= NG - 1:
                    act.wait_ge(S_["m_done"], s)
                    wait(act, "scan_done", s - 2, lo - 2)
                    act.activation(M[:, (lo - 1) % 2, :], M_ps[:, :], ACT.Identity, bias=b2_col[:, :]).then_inc(S_["m_evac"], 1)
                if lo >= 2 and hi - 2 <= NG - 1:
                    act.wait_ge(S_["st_done"], s - 1)
                    act.wait_ge(S_["released"], s - 1)
                    act.activation(ST[:, (lo - 2) % U, :, :].rearrange("p t f -> p (t f)"), ST_ps[:, :],
                                   ACT.Copy).then_inc(S_["st_evac"], 1)

            for s in range(U):
                group_step(s, s, s, 0)
            with act.Fori(1, R - 1) as i:
                for c in range(U):
                    group_step(i * U + c, U + c, (R - 2) * U + c, i)
            for s in range(NG - U, G_END):
                group_step(s, s, s, R - 1)

            def fin_copy(b, par, n, again):
                if again:
                    act.wait_ge(S_["fin_T"], b - 1)
                act.activation(outT_block[:, par, 0:n * P], outT[:, bass.ds(b * (BT * P), n * P)],
                               ACT.Copy).then_inc(S_["fin_copied"], 1)

            act.wait_ge(S_["acc_done"], NG)
            fin_copy(0, 0, BT, False)
            fin_copy(1, 1, BT, False)
            with act.Fori(1, (NB - 1) // 2) as i:
                for par in range(2):
                    fin_copy(i * 2 + par, par, BT, True)
            fin_copy(NB - 1, 0, 1, True)

        @block.tensor
        def _(pe):
            pe.wait_ge(S_["ident_ready"], 1)

            def columns(rows, half, name):
                for m in range(8):
                    k = 8 * half + m
                    i = pe.transpose(col_ps[half][:, m * R:(m + 1) * R], rows[:, k * P:(k + 1) * P], ident[0:R, 0:R])
                i.then_inc(S_[name], 1)

            pe.wait_ge(S_["src_f_ready"], 1)
            for half in range(2):
                columns(src_row_f, half, "src_T")
            pe.wait_ge(S_["wdiff_ready"], 1)

            def table_step(s, lo, hi, turn):
                if lo >= 3 and hi - 3 <= NB - 1:
                    n, par = tiles_of(lo - 3), (lo - 3) % 2
                    pe.wait_ge(S_["hT_done"], s - 2)
                    wait(pe, "q_evac", s - 4, lo - 4)
                    wait(pe, "p_evac", s - 4, lo - 4)
                    for t in range(n):
                        pe.matmul(p_ps[par][:, t * P:(t + 1) * P], hT_sb[:, par, t, :], w1_diff[:, :], start=True, stop=True)
                        i = pe.matmul(q_ps[par][:, t * P:(t + 1) * P], hT_sb[:, par, t, :], w1_sb[:, 1, :], start=True, stop=True)
                    i.then_inc(S_["pq_done"], 1)
                if lo >= 1 and hi - 1 <= NB - 1:
                    n, par = tiles_of(lo - 1), (lo - 1) % 2
                    pe.wait_ge(S_["h_act"], s)
                    if n > PA:
                        pe.wait_ge(S_["h_pool"], s)
                    wait(pe, "hT_done", s - 2, lo - 2)
                    for t in range(n):
                        i = pe.transpose(hT_ps[par][:, t * P:(t + 1) * P], h_sb[:, par, t, :], ident[:, :])
                    i.then_inc(S_["transp_done"], 1)

            for s in range(T_FIRST):
                table_step(s, s, s, 0)
            with pe.Fori(0, (T_BODY - T_FIRST) // 2) as i:
                for c in range(2):
                    table_step(i * 2 + (T_FIRST + c), T_FIRST + c, T_BODY - 2 + c, i)
            for s in range(T_BODY, T_END):
                table_step(s, s, s, 0)

            pe.wait_ge(S_["rel_last_ready"], 1)
            pe.wait_ge(S_["src_col_ready"], 2)
            for half in range(2):
                columns(rel_last, half, "rel_T")

            def broadcast_rel(c, s, lo):
                pe.matmul(rel_ps[:, :], ones[:, :], rowbuf[:, c, 0, :], start=True, stop=True).then_inc(S_["rel_done"], 1)

            pe.wait_ge(S_["q_evac"], NB)
            pe.wait_ge(S_["p_evac"], NB)
            pe.wait_ge(S_["rel_col_ready"], 2)
            pe.wait_ge(S_["bias_in"], 48)
            pe.wait_ge(row_in[0], 16)
            broadcast_rel(0, 0, 0)

            def group_step(s, lo, hi, turn):
                c = lo % U
                if hi <= NG - 1:
                    missing = 0 if lo < NG - 1 else GT_ - LAST_TILES
                    pe.wait_ge(gathered[c], (turn + 1) * (16 * GT_) - 16 * missing)
                    wait(pe, "sum_done", s, lo)
                    for t in range(GT_ if lo < NG - 1 else LAST_TILES):
                        i = pe.transpose(GT_ps[:, t * P:(t + 1) * P], G[:, c, t, :], ident[:, :])
                    i.then_inc(S_["gt_done"], 1)
                    pe.wait_ge(win_in[c], (turn + 1) * 16)
                    pe.wait_ge(S_["onehot_done"], s + 1)
                    wait(pe, "px_evac", s, lo)
                    pe.matmul(PX_ps[:, :], p_win[:, c, :], onehot[:, lo % 2, :], start=True, stop=True).then_inc(S_["px_done"], 1)
                if hi + 1 <= NG - 1:
                    nxt = (lo + 1) % U
                    pe.wait_ge(row_in[nxt], (turn + 1 + (1 if nxt == 0 else 0)) * 16)
                    broadcast_rel(nxt, s + 1, lo + 1)
                if lo >= 1 and hi - 1 <= NG - 1:
                    pe.wait_ge(S_["hidden_done"], s)
                    wait(pe, "m_evac", s - 1, lo - 1)
                    pe.matmul(M_ps[:, :], w2_sb[:, :], H[:, (lo - 1) % 2, :], start=True, stop=True).then_inc(S_["m_done"], 1)
                    wait(pe, "scan_done", s - 1, lo - 1)
                    pe.matmul(pen_ps[:, :], ones[:, :], rowbuf[:, (lo - 1) % U, 1, :],
                              start=True, stop=True).then_inc(S_["pen_done"], 1)
                if lo >= 2 and hi - 2 <= NG - 1:
                    pe.wait_ge(S_["scan_done"], s - 1)
                    wait(pe, "st_evac", s - 2, lo - 2)
                    for t in range(GT_):
                        i = pe.transpose(ST_ps[:, t * P:(t + 1) * P], S[:, (lo - 2) % 2, t * P:(t + 1) * P], ident[:, :])
                    i.then_inc(S_["st_done"], 1)
                if lo >= 3 and hi - 3 <= NG - 1:
                    pe.wait_ge(S_["st_evac"], s - 2)
                    pe.wait_ge(S_["L_done"], s - 2)
                    wait(pe, "acc_done", s - 3, lo - 3)
                    for t in range(GT_):
                        i = pe.matmul(sel_ps[:, 0:WN], ST[:, (lo - 3) % U, t, :], L[:, (lo - 3) % 2, t, :],
                                      start=(t == 0), stop=(t == GT_ - 1))
                    i.then_inc(S_["sel_done"], 1)

            for s in range(U):
                group_step(s, s, s, 0)
            with pe.Fori(1, R - 1) as i:
                for c in range(U):
                    group_step(i * U + c, U + c, (R - 2) * U + c, i)
            for s in range(NG - U, G_END):
                group_step(s, s, s, R - 1)

            def fin_transpose(b, par, n, again):
                pe.wait_ge(S_["fin_copied"], b + 1)
                if again:
                    pe.wait_ge(S_["fin_added"], b - 1)
                for t in range(n):
                    i = pe.transpose(fin_ps[par][:, t * P:(t + 1) * P], outT_block[:, par, t * P:(t + 1) * P], ident[:, :])
                i.then_inc(S_["fin_T"], 1)

            fin_transpose(0, 0, BT, False)
            fin_transpose(1, 1, BT, False)
            with pe.Fori(1, (NB - 1) // 2) as i:
                for par in range(2):
                    fin_transpose(i * 2 + par, par, BT, True)
            fin_transpose(NB - 1, 0, 1, True)

        @block.vector
        def _(dve):
            flat = lambda t: t[:, :, :].rearrange("r u e -> r (u e)")
            dve.memset(src_row[:, E_TAIL:RE], 0).then_inc(S_["edges_memset"], 1)
            dve.memset(flat(dst_row)[:, E_TAIL:RE], NO_NODE).then_inc(S_["edges_memset"], 1)
            dve.memset(flat(dst_next)[:, E_TAIL - 1:RE], NO_NODE).then_inc(S_["edges_memset"], 1)
            dve.memset(dst_before[:, :], -1).then_inc(S_["edges_memset"], 1)
            dve.memset(x_sb[:, NT - 1, :], 0.0).then_inc(S_["edges_memset"], 1)
            dve.memset(eps_col[:, :], EPS).then_inc(S_["dve_init"], 1)
            dve.memset(ones[:, :], 1.0).then_inc(S_["dve_init"], 1)
            dve.memset(end_row[:, NG - 1:NG], NO_NODE).then_inc(S_["dve_init"], 1)
            dve.wait_ge(S_["pool_init"], 4)
            dve.tensor_copy(iota_part[:, :], iota_part_i[:, :]).then_inc(S_["dve_init"], 1)
            dve.tensor_copy(iota_free1[:, :], iota_free_i[:, :]).then_inc(S_["dve_init"], 1)
            dve.memset(p_win[:, :, :], 0.0).then_inc(S_["loop_zeroed"], 1)
            dve.wait_ge(S_["weights_in"], 16)
            dve.tensor_tensor(w1_diff[:, :], w1_sb[:, 0, :], w1_sb[:, 1, :], ALU.subtract).then_inc(S_["wdiff_ready"], 1)
            dve.wait_ge(S_["x_block"], 16)

            def table_step(s, lo, hi, turn):
                before = lo >= 1 and hi - 1 <= NB - 1
                nb, pb = tiles_of(lo - 1), (lo - 1) % 2
                if before:
                    dve.wait_ge(S_["sqrt_done"], s)
                    wait(dve, "h_pool", s - 2, lo - 2)
                    dve.reciprocal(rstd[:, pb, 0:nb], std[:, pb, 0:nb]).then_inc(S_["rstd_done"], 1)
                if hi <= NB - 1:
                    n, par = tiles_of(lo), lo % 2
                    if lo == hi == 1:
                        dve.wait_ge(S_["x_first"], 16)
                    if lo == hi == X_FIRST:
                        dve.wait_ge(S_["x_rest"], 16)
                    if n == 1:
                        dve.wait_ge(S_["x_tail"], 16)
                    wait(dve, "mv_done", s - 1, lo - 1)
                    for t in range(n):
                        i = dve.bn_stats(stats[:, par, t, :], x_sb[:, bass.ds(s * BT + t, 1), :].rearrange("p o f -> p (o f)"))
                    i.then_inc(S_["stats_done"], 1)
                if before:
                    dve.wait_ge(S_["rstd_done"], s)
                    dve.scalar_tensor_tensor(neg_mean[:, pb, 0:nb], mean_var[:, pb, 0:nb, 0], -1.0, rstd[:, pb, 0:nb],
                                             ALU.mult, ALU.mult).then_inc(S_["nm_done"], 1)
                if hi <= NB - 1:
                    wait(dve, "nm_done", s - 1, lo - 1)
                    dve.wait_ge(S_["stats_done"], s + 1)
                    gate(dve)
                    for t in range(n):
                        i = dve.bn_aggr(mean_var[:, par, t, :], stats[:, par, t, :])
                    i.then_inc(S_["mv_done"], 1)
                if lo >= 4 and hi - 4 <= NB - 1:
                    n, par = tiles_of(lo - 4), (lo - 4) % 2
                    dve.wait_ge(S_["pq_done"], s - 3)
                    if hi - 4 >= 2:
                        dve.wait_ge(S_[f"p_stored{par}"], (turn + (lo - 4) // 2) * 16)
                    dve.tensor_copy(p_rows[:, par, 0:n, :].rearrange("p t n -> p (t n)"), p_ps[par][:, 0:n * P]
                                    ).then_inc(S_["p_evac"], 1)

            for s in range(T_FIRST):
                table_step(s, s, s, 0)
            with dve.Fori(0, (T_BODY - T_FIRST) // 2) as i:
                for c in range(2):
                    table_step(i * 2 + (T_FIRST + c), T_FIRST + c, T_BODY - 2 + c, i)
            for s in range(T_BODY, T_END):
                table_step(s, s, s, 0)

            dve.wait_ge(S_["base_in"], 32)
            dve.wait_ge(S_["dve_init"], 5)
            dve.tensor_tensor(wide_row[:, :], end_row[:, :], base_row[:, :], ALU.subtract).then_inc(S_["dve_small"], 1)
            dve.wait_ge(S_["dve_small"], 1)
            dve.tensor_scalar(end_row[:, :], wide_row[:, :], float(WN) - 0.5, None, ALU.is_ge).then_inc(S_["dve_small"], 1)
            dve.wait_ge(S_["dve_small"], 2)
            dve.reduce_max(any_wide_i[:, :], end_row[:, :], AX.X).then_inc(S_["anyw_ready"], 1)
            dve.wait_ge(S_["rel_i_ready"], 1)
            dve.tensor_scalar(wide[:, :], rel_i[:, :, GE - 1], float(WN) - 0.5, None, ALU.is_ge).then_inc(S_["wide_ready"], 1)
            dve.wait_ge(S_["wide_ready"], 1)
            dve.tensor_scalar(wide_off[:, :], wide[:, :], WIDE_OFF, None, ALU.mult).then_inc(S_["woff_ready"], 1)
            dve.wait_ge(S_["woff_ready"], 1)
            dve.tensor_tensor(rowpack[:, :, 0, :], rel_i[:, :, :],
                              wide_off[:, :].rearrange("r (u o) -> r u o", o=1).to_broadcast([R, U, GE]),
                              ALU.add).then_inc(S_["rel_row_ready"], 1)
            dve.wait_ge(S_["dst_in"], 32)
            dve.wait_ge(S_["dstn_in"], 32)
            dve.tensor_tensor(last[:, :].rearrange("r (u e) -> r u e", u=U), dst_row[:, :, :], dst_next[:, :, :],
                              ALU.not_equal).then_inc(S_["last_ready"], 1)
            dve.wait_ge(S_["before_in"], 16)
            dve.tensor_tensor(start[:, 0:1], dst_row[:, 0, 0:1], dst_before[:, :], ALU.not_equal).then_inc(S_["start_ready"], 1)
            dve.wait_ge(S_["last_ready"], 1)
            dve.tensor_scalar(rowpack[:, 0, 1, 1:GE], last[:, 0:GE - 1], PENALTY, None, ALU.mult)
            dve.tensor_scalar(rowpack[:, 1:U, 1, :], last[:, GE - 1:RE - 1].rearrange("r (u e) -> r u e", u=U - 1),
                              PENALTY, None, ALU.mult)
            dve.wait_ge(S_["start_ready"], 1)
            dve.tensor_scalar(rowpack[:, 0, 1, 0:1], start[:, 0:1], PENALTY, None, ALU.mult).then_inc(S_["pen_ready"], 1)
            dve.wait_ge(S_["rel_row_ready"], 1)
            dve.scalar_tensor_tensor(rel_last[:, :].rearrange("r (u e) -> r u e", u=U), rowpack[:, :, 0, :], 1.0,
                                     last[:, :].rearrange("r (u e) -> r u e", u=U), ALU.add, ALU.mult
                                     ).then_inc(S_["rel_last_ready"], 1)
            for half in range(2):
                dve.wait_ge(S_["rel_T"], half + 1)
                dve.tensor_copy(rel_last_col[:, :, 8 * half:8 * half + 8],
                                col_ps[half][:, 0:8 * R].rearrange("p (m r) -> p r m", m=8)).then_inc(S_["rel_col_ready"], 1)
            dve.wait_ge(S_["rel_col_ready"], 2)
            dve.wait_ge(S_["outT_zero"], 1)

            def one_hot(s, lo):
                dve.wait_ge(S_["rel_done"], s + 1)
                wait(dve, "px_done", s - 1, lo - 1)
                dve.tensor_scalar(onehot[:, lo % 2, :], rel_ps[:, :], iota_part[:, 0:1], None,
                                  ALU.is_equal).then_inc(S_["onehot_done"], 1)

            one_hot(0, 0)

            def group_step(s, lo, hi, turn):
                if hi <= NG - 1:
                    dve.wait_ge(S_["gt_done"], s + 1)
                    dve.wait_ge(S_["px_evac"], s + 1)
                    dve.tensor_tensor(px_sb[:, lo % 2, :], GT_ps[:, :], px_sb[:, lo % 2, :], ALU.add
                                      ).then_inc(S_["sum_done"], 1)
                if hi + 1 <= NG - 1:
                    one_hot(s + 1, lo + 1)
                if lo >= 1 and hi - 1 <= NG - 1:
                    dve.wait_ge(S_["m_evac"], s)
                    dve.wait_ge(S_["pen_done"], s)
                    wait(dve, "st_done", s - 2, lo - 2)
                    wait(dve, "scan_done", s - 1, lo - 1)
                    k = (lo - 1) % 2
                    initial = 0.0 if lo == 1 else S[:, 1 - k, GE - 1:GE]
                    dve.tensor_tensor_scan(S[:, k, :], pen_ps[:, :], M[:, k, :], initial, ALU.add, ALU.max
                                           ).then_inc(S_["scan_done"], 1)
                if lo >= 2 and hi - 2 <= NG - 1:
                    wait(dve, "sel_done", s - 3, lo - 3)
                    row = (lo - 2) // U if lo == hi else (turn - 1 if lo % U < 2 else turn)
                    for t in range(GT_):
                        m = ((lo - 2) % U) * GT_ + t
                        i = dve.tensor_scalar(L[:, (lo - 2) % 2, t, :], iota_free1[:, 0:WN],
                                              rel_last_col[:, bass.ds(row, 1), m:m + 1].rearrange("p o t -> p (o t)"),
                                              None, ALU.is_equal)
                    i.then_inc(S_["L_done"], 1)
                if lo >= 3 and hi - 3 <= NG - 1:
                    base = dve.value_load(base_row[0:1, bass.ds(s - 3, 1)], min_val=0, max_val=N - 1)
                    dve.wait_ge(S_["sel_done"], s - 2)
                    wait(dve, "acc_done", s - 3, lo - 3)
                    dve.tensor_tensor(outT[:, bass.ds(base, WN)], outT[:, bass.ds(base, WN)], sel_ps[:, 0:WN],
                                      ALU.add).then_inc(S_["acc_done"], 1)

            for s in range(U):
                group_step(s, s, s, 0)
            with dve.Fori(1, R - 1) as i:
                for c in range(U):
                    group_step(i * U + c, U + c, (R - 2) * U + c, i)
            for s in range(NG - U, G_END):
                group_step(s, s, s, R - 1)

            dve.wait_ge(S_["wide_merged"], 1)

            def fin_add(b, par, n):
                dve.wait_ge(S_["fin_T"], b + 1)
                tiles = x_sb[:, bass.ds(b * BT, n), :].rearrange("p t f -> p (t f)")
                dve.tensor_tensor(tiles, tiles, fin_ps[par][:, 0:n * P], ALU.add).then_inc(S_["fin_added"], 1)

            with dve.Fori(0, (NB - 1) // 2) as i:
                for par in range(2):
                    fin_add(i * 2 + par, par, BT)
            fin_add(NB - 1, 0, 1)


_INS = ['x', 'src', 'dst', 'L0_gnn_W1', 'L0_gnn_b1', 'L0_gnn_W2', 'L0_gnn_b2']


def kernel(**inputs):
    import numpy as _np
    import concourse.bacc as _bacc
    from concourse import mybir as _mybir
    from concourse.bass_utils import run_bass_kernel_spmd as _run

    nc = _bacc.Bacc("TRN2", target_bir_lowering=False, num_devices=1)
    arrays, args = {}, []
    for name in _INS:
        a = _np.ascontiguousarray(inputs[name])
        arrays[f"in_{name}_dram"] = a
        args.append(nc.dram_tensor(f"in_{name}_dram", a.shape, _mybir.dt.from_np(a.dtype), kind="ExternalInput").ap())
    shape = inputs["x"].shape
    args.append(nc.dram_tensor("out_0_dram", shape, _mybir.dt.float32, kind="ExternalOutput").ap())
    gnn_kernel(nc, *args)
    r = _run(nc, [arrays], core_ids=[0])
    return r.results[0]["out_0_dram"]
```

```python
from contextlib import ExitStack

import concourse.bass as bass
from concourse import mybir


def gnn_kernel(nc, x, src, dst, w1, b1, w2, b2, out):
    f32, bf16, i32 = mybir.dt.float32, mybir.dt.bfloat16, mybir.dt.int32
    ALU, ACT, AX = mybir.AluOpType, mybir.ActivationFunctionType, mybir.AxisListType

    N, F = x.shape
    E = src.shape[0]
    P = 128
    GE = 512
    WN = 64
    GT_ = GE // P
    U = 4
    RE = U * GE
    R = -(-E // RE)
    NG = R * U
    E_FULL = (R - 1) * RE
    E_TAIL = E - E_FULL
    NT = -(-N // P)
    N_FULL = (NT - 1) * P
    N_TAIL = N - N_FULL
    BT = 4
    NB = -(-NT // BT)
    LAST_TILES = -(-(E - (NG - 1) * GE) // P)
    assert 0 < LAST_TILES <= GT_
    assert NT == (NB - 1) * BT + 1 and (NB - 1) % U == 0 and 0 < E_TAIL < RE and N_TAIL > 0
    NPAD = (NT + 1) * P
    NO_NODE = N
    WIDE_OFF = 1024.0
    NO_SCATTER = 20000.0
    PENALTY = -3.0e38
    EPS = 1e-5

    EARLY = NB - 2
    EARLY_TURN = R - 2 - EARLY
    EARLY_END = EARLY_TURN + EARLY
    assert 1 < EARLY_TURN and EARLY_END < R - 1 and EARLY % 2 == 1

    q_table = nc.dram_tensor("q_table", (N, F), f32, kind="Internal").ap()
    p_table = nc.dram_tensor("p_table", (NPAD, F), f32, kind="Internal").ap()
    rows_dram = nc.dram_tensor("rows_dram", (R, U * 2 * GE), bf16, kind="Internal").ap()
    p_index = nc.dram_tensor("p_index", (R, RE), i32, kind="Internal").ap()
    s_index = nc.dram_tensor("s_index", (R, RE), i32, kind="Internal").ap()
    wide_out = nc.dram_tensor("wide_out", (NT * P, F), f32, kind="Internal").ap()

    ctx = ExitStack()
    with ctx:
        def sb(name, shape, dt):
            return ctx.enter_context(nc.sbuf_tensor(name, shape, dt))

        def sem(name):
            return ctx.enter_context(nc.semaphore(name))

        ident = sb("ident", [P, P], f32)
        ones = sb("ones", [P, P], bf16)
        iota_part_i = sb("iota_part_i", [P, 1], i32)
        iota_part = sb("iota_part", [P, 1], f32)
        iota_free_i = sb("iota_free_i", [P, P], i32)
        iota_free1 = sb("iota_free1", [P, P], f32)
        eps_col = sb("eps_col", [P, 1], f32)
        w1_sb = sb("w1_sb", [P, 2, F], f32)
        w1_diff = sb("w1_diff", [P, F], f32)
        w2_sb = sb("w2_sb", [P, F], f32)
        b1_col = sb("b1_col", [P, 1], f32)
        b2_col = sb("b2_col", [P, 1], f32)
        zeros = sb("zeros", [P, F], f32)
        x_sb = sb("x_sb", [P, NT, F], f32)
        stats = sb("stats", [P, 2, BT, 6], f32)
        mean_var = sb("mean_var", [P, 2, BT, 2], f32)
        std = sb("std", [P, 2, BT], f32)
        rstd = sb("rstd", [P, 2, BT], f32)
        neg_mean = sb("neg_mean", [P, 2, BT], f32)
        h_sb = sb("h_sb", [P, 2, BT, F], f32)
        hT_sb = sb("hT_sb", [P, NT, P], f32)
        q_rows = sb("q_rows", [P, 2, BT, F], f32)
        q_last = sb("q_last", [P, F], f32)
        outT = sb("outT", [P, NPAD], f32)
        outT_block = sb("outT_block", [P, 2, BT * P], f32)
        src_row = sb("src_row", [R, RE], i32)
        src_row_f = sb("src_row_f", [R, RE], f32)
        rel_last = src_row_f
        dst_row = sb("dst_row", [R, U, GE], i32)
        dst_next = sb("dst_next", [R, U, GE], i32)
        dst_before = sb("dst_before", [R, 1], i32)
        rel_i = sb("rel_i", [R, U, GE], i32)
        last = sb("last", [R, RE], f32)
        wide = sb("wide", [R, U], f32)
        wide_off = sb("wide_off", [R, U], f32)
        start = sb("start", [R, 1], f32)
        rowpack = sb("rowpack", [R, U, 2, GE], bf16)
        base_row = sb("base_row", [1, NG], i32)
        end_row = sb("end_row", [1, NG], i32)
        wide_row = sb("wide_row", [1, NG], f32)
        any_wide_i = sb("any_wide_i", [1, 1], i32)
        block_end = sb("block_end", [1, EARLY], f32)
        short = sb("short", [1, EARLY], f32)
        late = sb("late", [1, 1], f32)
        early_i = sb("early_i", [1, 1], i32)
        src_col = sb("src_col", [P, R, U * GT_], i32)
        rel_last_col = sb("rel_last_col", [P, R, U * GT_], f32)
        idx = sb("idx", [P, U, GT_], i32)
        G = sb("G", [P, U, GT_, F], f32)
        p_win = sb("p_win", [P, U, F], f32)
        rowbuf = sb("rowbuf", [P, U, 2, GE], bf16)
        onehot = sb("onehot", [P, 2, GE], f32)
        px_sb = sb("px_sb", [P, 2, GE], f32)
        H = sb("H", [P, 2, GE], f32)
        M = sb("M", [P, 2, GE], f32)
        S = sb("S", [P, 2, GE], f32)
        L = sb("L", [P, 2, GT_, WN], f32)
        ST = sb("ST", [P, U, GT_, F], f32)
        idx_p = sb("idx_p", [P, U, GT_], i32)
        idx_s = sb("idx_s", [P, U, GT_], i32)

        bank = [ctx.enter_context(nc.psum_tensor(f"bank{i}", [P, GE], f32)) for i in range(8)]
        hT_ps, q_act_ps, q_ps = bank[0:2], bank[2:4], bank[4:6]
        p_ps = bank[2:4]
        col_ps = bank[6:8]
        GT_ps, PX_ps, rel_ps, pen_ps, M_ps, ST_ps, sel_ps = bank[0:7]
        fin_ps = bank[0:2]
        early_ps = bank[7]

        S_ = {n: sem(n) for n in """
            loop_zeroed h_pool h_scaled dve_init pool_init ident_ready weights_in wdiff_ready
            src_in dst_in dstn_in before_in before_main edges_memset base_in bias_in
            x_in0 x_in1 x_in2 x_in3 x_in4
            sqrt_warm stats_done mv_done sqrt_done rstd_done nm_done h_act transp_done hT_done q_done q_evac q_evac_act p_done p_evac
            q_stored0 q_stored1 p_stored0 p_stored1 p_stored2 p_stored3 p_zero
            src_f_ready src_T src_col_ready rel_i_ready last_ready wide_ready woff_ready
            rel_row_ready rel_last_ready start_ready pen_ready rel_T rel_col_ready rows_stored anyw_ready early_ready dve_small
            idx_staged rel_done onehot_done gt_done px_done px_evac gates sum_done hidden_done m_done m_evac
            pen_done scan_done st_done st_evac L_done sel_done acc_done
            released wide_merged fin_copied fin_T fin_added out_stored outT_zero
            slow_v slow_store slow_idx slow_gather slow_scatter slow_zero
            """.split()}
        gathered = [sem(f"gathered{c}") for c in range(U)]
        win_in = [sem(f"win_in{c}") for c in range(U)]
        row_in = [sem(f"row_in{c}") for c in range(U)]

        def wait(eng, name, value, least):
            if least > 0:
                eng.wait_ge(S_[name] if isinstance(name, str) else name, value)

        def gate(eng):
            eng.sem_inc(S_["gates"], 1)

        T_END = NB + 3
        QD = 2
        PA = 2
        X_CUTS = [0, 1, 3, 5, 8, NB]
        QUARTER = RE // 4
        P_SLOTS = U
        G_END = NG + 3

        def tiles_of(b):
            return 1 if b == NB - 1 else BT

        def p_table_stored(eng):
            for c in range(P_SLOTS):
                eng.wait_ge(S_[f"p_stored{c}"], 16 * ((NB - 1) // P_SLOTS + (1 if c == 0 else 0)))

        block = ctx.enter_context(nc.Block())

        @block.sync
        def _(sp):
            src_full = src[0:E_FULL].rearrange("(r e) -> r e", e=RE)
            src_tail = src[E_FULL:E].rearrange("(r e) -> r e", r=1)
            tiles = x[0:N_FULL, :].rearrange("(t p) f -> p t f", p=P)

            def load_x(k):
                first, end = X_CUTS[k] * BT, min(X_CUTS[k + 1] * BT, NT - 1)
                sp.dma_start(x_sb[:, first:end, :], tiles[:, first:end, :]).then_inc(S_[f"x_in{k}"], 16)

            load_x(0)
            load_x(1)
            sp.wait_ge(S_["edges_memset"], 5)
            sp.dma_start(src_row[0:R - 1, :], src_full).then_inc(S_["src_in"], 16)
            sp.dma_start(src_row[R - 1:R, 0:E_TAIL], src_tail).then_inc(S_["src_in"], 16)
            load_x(2)
            sp.dma_start(w1_sb[:, :, :], w1.rearrange("(a k) f -> k a f", a=2)).then_inc(S_["weights_in"], 16)
            load_x(3)
            load_x(4)
            sp.dma_start(x_sb[0:N_TAIL, NT - 1, :], x[N_FULL:N, :]).then_inc(S_["x_in4"], 16)
            dst_full = dst[0:E_FULL].rearrange("(r e) -> r e", e=RE)
            dst_tail = dst[E_FULL:E].rearrange("(r e) -> r e", r=1)
            dst_flat = dst_row[:, :, :].rearrange("r u e -> r (u e)")
            sp.dma_start(dst_flat[0:R - 1, :], dst_full).then_inc(S_["dst_in"], 16)
            sp.dma_start(dst_flat[R - 1:R, 0:E_TAIL], dst_tail).then_inc(S_["dst_in"], 16)
            next_flat = dst_next[:, :, :].rearrange("r u e -> r (u e)")
            sp.dma_start(next_flat[0:R - 1, :], dst[1:E_FULL + 1].rearrange("(r e) -> r e", e=RE)).then_inc(S_["dstn_in"], 16)
            sp.dma_start(next_flat[R - 1:R, 0:E_TAIL - 1],
                         dst[E_FULL + 1:E].rearrange("(r e) -> r e", r=1)).then_inc(S_["dstn_in"], 16)
            sp.dma_start(w2_sb[:, :], w2).then_inc(S_["bias_in"], 16)
            sp.dma_start(b1_col[:, :], b1.rearrange("(k a) -> k a", a=1)).then_inc(S_["bias_in"], 16)
            sp.dma_start(b2_col[:, :], b2.rearrange("(k a) -> k a", a=1)).then_inc(S_["bias_in"], 16)
            with nc.allow_non_contiguous_dma(reason="one number of each group or row"):
                sp.dma_start(dst_before[1:R, :], bass.AP(dst.tensor, RE - 1, [[RE, R - 1], [1, 1]])).then_inc(S_["before_in"], 16)
                sp.dma_start(base_row[:, :], bass.AP(dst.tensor, 0, [[GE * NG, 1], [GE, NG]])).then_inc(S_["base_in"], 16)
                sp.dma_start(end_row[:, 0:NG - 1], bass.AP(dst.tensor, GE - 1, [[GE * NG, 1], [GE, NG - 1]])).then_inc(S_["base_in"], 16)
            sp.wait_ge(S_["pool_init"], 1)
            sp.dma_start(p_table[N:N_FULL + P, :], zeros[0:P - N_TAIL, :]).then_inc(S_["p_zero"], 16)
            sp.dma_start(p_table[N_FULL + P:NPAD, :], zeros[:, :]).then_inc(S_["p_zero"], 16)

            def store_blocks(name, table, rows_sb, slots, first, end):
                with sp.Fori(first, end) as i:
                    for c in range(slots):
                        b = i * slots + c
                        sp.wait_ge(S_[f"{name}_evac"], b + 1)
                        if name == "q":
                            sp.wait_ge(S_["q_evac_act"], b + 1)
                        sp.dma_start(table[bass.ds(b * (BT * P), BT * P), :].rearrange("(t p) f -> p t f", p=P),
                                     rows_sb[:, c, :, :]).then_inc(S_[f"{name}_stored{c}"], 16)

            store_blocks("q", q_table, q_rows, 2, 0, (NB - 1) // 2)
            sp.wait_ge(S_["q_evac"], NB)
            sp.dma_start(q_table[N_FULL:N, :], q_last[0:N_TAIL, :]).then_inc(S_["q_stored0"], 16)
            turns = (NB - 1) // P_SLOTS
            store_blocks("p", p_table, ST, P_SLOTS, 0, turns - 1)
            sp.wait_ge(S_["rel_row_ready"], 1)
            sp.wait_ge(S_["pen_ready"], 1)
            sp.dma_start(rows_dram[:, :], rowpack[:, :, :, :].rearrange("r u a e -> r (u a e)")).then_inc(S_["rows_stored"], 16)
            store_blocks("p", p_table, ST, P_SLOTS, turns - 1, turns)
            sp.wait_ge(S_["p_evac"], NB)
            sp.dma_start(p_table[N_FULL:N, :], ST[0:N_TAIL, 0, 0, :]).then_inc(S_["p_stored0"], 16)

            sp.wait_ge(S_["rows_stored"], 16)
            sp.wait_ge(S_["loop_zeroed"], 2)
            rows_by_turn = rows_dram.rearrange("r (u c) -> r u c", u=U)

            def load_row(i, c):
                sp.dma_start(rowbuf[0:1, c, :, :].rearrange("o a e -> o (a e)"),
                             rows_by_turn[bass.ds(i, 1), c, :]).then_inc(row_in[c], 16)

            def load_window(i, c):
                base = sp.value_load(base_row[0:1, bass.ds(i * U + c, 1)], min_val=0, max_val=N - 1)
                sp.dma_start(p_win[0:WN, c, :], p_table[bass.ds(base, WN), :]).then_inc(win_in[c], 16)

            def load_turn(i):
                for c in range(U):
                    sp.wait_ge(S_["px_done"], i * U + (c - U + 1))
                    load_window(i, c)
                    sp.wait_ge(S_["pen_done"], i * U + (c - U + 1))
                    load_row(i, c)

            for c in range(U):
                load_row(0, c)
            sp.wait_ge(S_["p_zero"], 32)
            p_table_stored(sp)
            sp.wait_ge(S_["base_in"], 32)
            for c in range(U):
                load_window(0, c)
            sp.wait_ge(S_["early_ready"], 1)
            early = sp.value_load(early_i[0:1, 0:1], min_val=0, max_val=1)
            with sp.Fori(1, EARLY_TURN + 1) as i:
                load_turn(i)

            def store_block(b):
                sp.wait_ge(S_["fin_added"], b + 1)
                sp.dma_start(out[bass.ds(b * (BT * P), BT * P), :].rearrange("(t p) f -> p t f", p=P),
                             x_sb[:, bass.ds(b * BT, BT), :]).then_inc(S_["out_stored"], 16)

            with sp.If(early > 0):
                with sp.Fori(EARLY_TURN + 1, EARLY_END + 1) as i:
                    load_turn(i)
                    store_block(i - (EARLY_TURN + 1))
            with sp.Else():
                with sp.Fori(EARLY_TURN + 1, EARLY_END + 1) as i:
                    load_turn(i)
            with sp.Fori(EARLY_END + 1, R) as i:
                load_turn(i)
            with sp.If(early < 1):
                with sp.Fori(0, EARLY) as b:
                    store_block(b)
            for b in range(EARLY, NB - 1):
                store_block(b)
            sp.wait_ge(S_["fin_added"], NB)
            sp.dma_start(out[N_FULL:N, :], x_sb[0:N_TAIL, NT - 1, :]).then_inc(S_["out_stored"], 16)
            sp.wait_ge(S_["out_stored"], 16 * NB)

        @block.gpsimd
        def _(pool):
            pool.memset(zeros[:, :], 0.0).then_inc(S_["pool_init"], 1)
            pool.memset(ident[:, :], 0.0).then_inc(S_["pool_init"], 1)
            pool.iota(iota_part_i[:, :], pattern=[[0, 1]], base=0, channel_multiplier=1).then_inc(S_["pool_init"], 1)
            pool.iota(iota_free_i[:, :], pattern=[[1, P]], base=1, channel_multiplier=0).then_inc(S_["pool_init"], 1)
            pool.wait_ge(S_["pool_init"], 2)
            pool.affine_select(out=ident[:, :], in_=ident[:, :], compare_op=ALU.not_equal, fill=1.0, base=0,
                               pattern=[[-1, P]], channel_multiplier=1).then_inc(S_["ident_ready"], 1)
            pool.memset(rowbuf[:, :, :, :], 0.0).then_inc(S_["loop_zeroed"], 1)

            def normalise(s, par, turn):
                n = BT - PA
                h = h_sb[:, par, PA:BT, :]
                spread = lambda t: t[:, par, PA:BT].rearrange("p (t o) -> p t o", o=1).to_broadcast([P, n, F])
                pool.wait_ge(S_["nm_done"], s + 1)
                if par + 2 * turn >= 2 if isinstance(turn, int) else True:
                    pool.wait_ge(S_["transp_done"], s - 1)
                gate(pool)
                pool.tensor_tensor(h, x_sb[:, bass.ds(s * BT + PA, n), :], spread(rstd), ALU.mult).then_inc(S_["h_scaled"], 1)
                pool.wait_ge(S_["h_scaled"], s + 1)
                gate(pool)
                pool.tensor_tensor(h, h, spread(neg_mean), ALU.add).then_inc(S_["h_pool"], 1)

            for par in range(2):
                normalise(par, par, 0)
            with pool.Fori(1, (NB - 1) // 2) as i:
                for par in range(2):
                    normalise(i * 2 + par, par, i)
            pool.wait_ge(S_["weights_in"], 16)
            pool.tensor_tensor(w1_diff[:, :], w1_sb[:, 0, :], w1_sb[:, 1, :], ALU.subtract).then_inc(S_["wdiff_ready"], 1)
            pool.wait_ge(S_["dst_in"], 32)
            pool.tensor_tensor(rel_i[:, :, :], dst_row[:, :, :], dst_row[:, :, 0:1].to_broadcast([R, U, GE]),
                               ALU.subtract).then_inc(S_["rel_i_ready"], 1)
            pool.wait_ge(S_["anyw_ready"], 1)
            any_wide = pool.value_load(any_wide_i[0:1, 0:1], min_val=0, max_val=1)
            pool.wait_ge(S_["q_stored0"], 16 * ((NB - 1) // 2 + 1))
            pool.wait_ge(S_["q_stored1"], 16 * ((NB - 1) // 2))

            def gather(i, c, again, signal, tiles=GT_):
                pool.wait_ge(S_["idx_staged"], i * U + (c + 1))
                if again:
                    pool.wait_ge(S_["gt_done"], i * U + (c - U + 1))
                gate(pool)
                for t in range(tiles):
                    pool.indirect_dma_start(G[:, c, t, :], None, q_table[:, :],
                                            bass.IndirectOffsetOnAxis(ap=idx[:, c, t:t + 1], axis=0)).then_inc(signal, 16)

            def slow_setup():
                v = [0]

                def chain(instruction):
                    v[0] += 1
                    instruction.then_inc(S_["slow_v"], 1)
                    pool.wait_ge(S_["slow_v"], v[0])

                pool.dma_start(wide_out.rearrange("(t p) f -> p t f", p=P),
                               zeros[:, :].rearrange("p (a f) -> p a f", a=1).to_broadcast([P, NT, F])).then_inc(S_["slow_zero"], 16)
                pool.wait_ge(S_["rel_T"], 2)
                pool.wait_ge(S_["wide_ready"], 1)
                d, a = src_row_f, src_row
                by_group = lambda t: t[:, :].rearrange("r (u e) -> r u e", u=U)
                spread = wide[:, :].rearrange("r (u o) -> r u o", o=1).to_broadcast([R, U, GE])
                chain(pool.tensor_copy(d[:, :], dst_row[:, :, :].rearrange("r u e -> r (u e)")))
                chain(pool.tensor_scalar(d[:, :], d[:, :], -float(NO_NODE), None, ALU.add))
                chain(pool.tensor_tensor(by_group(d), by_group(d), spread, ALU.mult))
                chain(pool.tensor_scalar(a[:, :], d[:, :], float(NO_NODE), None, ALU.add))
                pool.dma_start(p_index[:, :], a[:, :]).then_inc(S_["slow_store"], 16)
                pool.wait_ge(S_["slow_store"], 16)
                chain(pool.tensor_copy(d[:, :], dst_row[:, :, :].rearrange("r u e -> r (u e)")))
                chain(pool.tensor_scalar(d[:, :], d[:, :], -NO_SCATTER, None, ALU.add))
                chain(pool.tensor_tensor(by_group(d), by_group(d), spread, ALU.mult))
                pool.wait_ge(S_["last_ready"], 1)
                chain(pool.tensor_tensor(d[:, :], d[:, :], last[:, :], ALU.mult))
                chain(pool.tensor_scalar(a[:, :], d[:, :], NO_SCATTER, None, ALU.add))
                pool.dma_start(s_index[:, :], a[:, :]).then_inc(S_["slow_store"], 16)
                pool.wait_ge(S_["slow_store"], 32)
                pool.wait_ge(S_["slow_zero"], 16)
                pool.wait_ge(S_["p_zero"], 32)
                p_table_stored(pool)

            p_cols = p_index.rearrange("r (u t p) -> p (r u) t", p=P, t=GT_)
            s_cols = s_index.rearrange("r (u t p) -> p (r u) t", p=P, t=GT_)

            def slow_gather(i, c, again, tiles=GT_):
                j = i * U + c
                if again:
                    pool.wait_ge(S_["slow_scatter"], (j - (U - 1)) * (16 * GT_))
                with nc.allow_non_contiguous_dma(reason="an index per partition"):
                    gate(pool)
                    pool.dma_start(idx_p[:, c, :].rearrange("p (o t) -> p o t", o=1),
                                   p_cols[:, bass.ds(j, 1), :]).then_inc(S_["slow_idx"], 16)
                    pool.wait_ge(S_["slow_idx"], (j * 2 + 1) * 16)
                    gate(pool)
                    pool.dma_start(idx_s[:, c, :].rearrange("p (o t) -> p o t", o=1),
                                   s_cols[:, bass.ds(j, 1), :]).then_inc(S_["slow_idx"], 16)
                    pool.wait_ge(S_["slow_idx"], (j * 2 + 2) * 16)
                gather(i, c, again, S_["slow_gather"], tiles)
                pool.wait_ge(S_["slow_gather"], (j + 1) * (16 * GT_) - 16 * (GT_ - tiles))
                gate(pool)
                for t in range(tiles):
                    pool.indirect_dma_start(G[:, c, t, :], None, p_table[:, :],
                                            bass.IndirectOffsetOnAxis(ap=idx_p[:, c, t:t + 1], axis=0),
                                            compute_op=ALU.add).then_inc(gathered[c], 16)

            def slow_scatter(i, c):
                j = i * U + c
                pool.wait_ge(S_["st_evac"], j + 1)
                gate(pool)
                for t in range(GT_):
                    pool.indirect_dma_start(wide_out[:, :], bass.IndirectOffsetOnAxis(ap=idx_s[:, c, t:t + 1], axis=0),
                                            ST[:, c, t, :], None, bounds_check=N - 1, oob_is_err=False
                                            ).then_inc(S_["slow_scatter"], 16)
                pool.wait_ge(S_["slow_scatter"], (j + 1) * (16 * GT_))
                pool.sem_inc(S_["released"], 1)

            pool.sem_inc(S_["released"], U)
            with pool.If(any_wide > 0):
                slow_setup()
                for c in range(U):
                    slow_gather(0, c, False)
                with pool.Fori(1, R - 1) as i:
                    for c in range(U):
                        slow_scatter(i - 1, c)
                        slow_gather(i, c, True)
                for c in range(U):
                    slow_scatter(R - 2, c)
                    slow_gather(R - 1, c, True, GT_ if c < U - 1 else LAST_TILES)
                for c in range(U):
                    slow_scatter(R - 1, c)
                pool.dma_start(x_sb[:, :, :], wide_out.rearrange("(t p) f -> p t f", p=P),
                               accum_op=ALU.add).then_inc(S_["slow_zero"], 16)
                pool.wait_ge(S_["slow_zero"], 32)
                pool.sem_inc(S_["wide_merged"], 1)
            with pool.Else():
                pool.sem_inc(S_["released"], NG)
                for c in range(U):
                    gather(0, c, False, gathered[c])
                with pool.Fori(1, R - 1) as i:
                    for c in range(U):
                        gather(i, c, True, gathered[c])
                for c in range(U):
                    gather(R - 1, c, True, gathered[c], GT_ if c < U - 1 else LAST_TILES)
                pool.sem_inc(S_["wide_merged"], 1)

        @block.scalar
        def _(act):
            act.wait_ge(S_["dve_init"], 1)
            act.activation(std[:, 0, 0:1], eps_col[:, :], ACT.Sqrt).then_inc(S_["sqrt_warm"], 1)

            def clear_outT(first, end):
                act.activation(outT[:, first:end].rearrange("p (t f) -> p t f", f=F),
                               zeros[:, :].rearrange("p (a f) -> p a f", a=1).to_broadcast([P, (end - first) // F, F]),
                               ACT.Copy).then_inc(S_["outT_zero"], 1)

            HALF = NB // 2 * BT * P
            act.wait_ge(S_["pool_init"], 1)
            clear_outT(0, HALF)

            def table_step(s):
                if 1 <= s <= NB:
                    b, par = s - 1, (s - 1) % 2
                    act.wait_ge(S_["nm_done"], b + 1)
                    wait(act, "transp_done", b - 1, b - 1)
                    for t in range(min(PA, tiles_of(b))):
                        i = act.activation(h_sb[:, par, t, :], x_sb[:, b * BT + t, :], ACT.Identity,
                                           bias=neg_mean[:, par, t:t + 1], scale=rstd[:, par, t:t + 1])
                    i.then_inc(S_["h_act"], 1)
                if s <= NB - 1:
                    act.wait_ge(S_["mv_done"], s + 1)
                    wait(act, "nm_done", s - 1, s - 1)
                    act.activation(std[:, s % 2, 0:tiles_of(s)], mean_var[:, s % 2, 0:tiles_of(s), 1], ACT.Sqrt,
                                   bias=eps_col[:, :]).then_inc(S_["sqrt_done"], 1)
                if 2 <= s <= NB + 1:
                    b = s - 2
                    n = tiles_of(b)
                    act.wait_ge(S_["transp_done"], b + 1)
                    act.activation(hT_sb[:, b * BT:b * BT + n, :].rearrange("p t n -> p (t n)"), hT_ps[b % 2][:, 0:n * P],
                                   ACT.Relu).then_inc(S_["hT_done"], 1)
                if 3 <= s <= NB + 1:
                    b = s - 3
                    act.wait_ge(S_["q_done"], b + 1)
                    wait(act, f"q_stored{b % 2}", b // 2 * 16, b // 2)
                    act.activation(q_rows[:, b % 2, QD:BT, :].rearrange("p t n -> p (t n)"), q_act_ps[b % 2][:, QD * P:BT * P],
                                   ACT.Copy).then_inc(S_["q_evac_act"], 1)

            act.wait_ge(S_["sqrt_warm"], 1)
            for s in range(T_END - 1):
                table_step(s)
                for k in {1: (0, 1), 2: (2,), 3: (3,)}.get(s, ()):
                    act.wait_ge(S_["src_in"], 32)
                    k *= QUARTER
                    act.activation(src_row_f[:, k:k + QUARTER], src_row[:, k:k + QUARTER], ACT.Copy).then_inc(S_["src_f_ready"], 1)
                if NB <= s + 1 <= NB + 1:
                    half = s + 1 - NB
                    m = 8 * half
                    act.wait_ge(S_["src_T"], half + 1)
                    act.activation(src_col[:, :, m:m + 8],
                                   col_ps[half][:, 0:8 * R].rearrange("p (m r) -> p r m", m=8),
                                   ACT.Copy).then_inc(S_["src_col_ready"], 1)
            act.wait_ge(S_["src_col_ready"], 2)
            act.wait_ge(S_["bias_in"], 48)

            def stage_index(j, c, k):
                r = j // U if isinstance(j, int) else k
                act.activation(idx[:, c, :].rearrange("p (o t) -> p o t", o=1),
                               src_col[:, bass.ds(r, 1), c * GT_:(c + 1) * GT_], ACT.Copy).then_inc(S_["idx_staged"], 1)

            for c in range(U):
                stage_index(c, c, None)
            def p_copy(b, c, n, turn):
                act.wait_ge(S_["p_done"], b + 1)
                if turn is not None:
                    act.wait_ge(S_[f"p_stored{c}"], turn * 16)
                act.activation(ST[:, c, 0:n, :].rearrange("p t n -> p (t n)"), p_ps[c % 2][:, 0:n * P],
                               ACT.Copy).then_inc(S_["p_evac"], 1)

            for c in range(P_SLOTS):
                p_copy(c, c, BT, None)
            with act.Fori(1, (NB - 1) // P_SLOTS) as i:
                for c in range(P_SLOTS):
                    p_copy(i * P_SLOTS + c, c, BT, i)
            p_copy(NB - 1, 0, 1, (NB - 1) // P_SLOTS)
            clear_outT(HALF, NPAD)
            p_table_stored(act)

            def group_step(s, lo, hi, turn):
                if hi + U <= NG - 1:
                    c = lo % U
                    act.wait_ge(gathered[c], (turn + 1) * (16 * GT_))
                    stage_index(s + U, c, turn + 1)
                if lo >= 1 and hi - 1 <= NG - 1:
                    act.wait_ge(S_["sum_done"], s)
                    wait(act, "m_done", s - 2, lo - 2)
                    act.activation(H[:, (lo - 1) % 2, :], px_sb[:, (lo - 1) % 2, :], ACT.Relu).then_inc(S_["hidden_done"], 1)
                if hi <= NG - 1:
                    wait(act, "hidden_done", s - 1, lo - 1)
                    act.wait_ge(S_["px_done"], s + 1)
                    act.activation(px_sb[:, lo % 2, :], PX_ps[:, :], ACT.Identity, bias=b1_col[:, :]).then_inc(S_["px_evac"], 1)
                if lo >= 1 and hi - 1 <= NG - 1:
                    act.wait_ge(S_["m_done"], s)
                    wait(act, "scan_done", s - 2, lo - 2)
                    act.activation(M[:, (lo - 1) % 2, :], M_ps[:, :], ACT.Identity, bias=b2_col[:, :]).then_inc(S_["m_evac"], 1)
                if lo >= 2 and hi - 2 <= NG - 1:
                    act.wait_ge(S_["st_done"], s - 1)
                    act.wait_ge(S_["released"], s - 1)
                    act.activation(ST[:, (lo - 2) % U, :, :].rearrange("p t f -> p (t f)"), ST_ps[:, :],
                                   ACT.Copy).then_inc(S_["st_evac"], 1)

            def group_turns(first, end, output=False):
                with act.Fori(first, end) as i:
                    for c in range(U):
                        group_step(i * U + c, U + c, (R - 2) * U + c, i)
                        if output and c == 1:
                            act.wait_ge(S_["acc_done"], i * U - U)
                            fin_copy(i - EARLY_TURN, 0, BT, False)
                        if output and c == U - 1:
                            act.wait_ge(S_["fin_T"], i - (EARLY_TURN - 1))

            def fin_copy(b, par, n, again):
                if again:
                    act.wait_ge(S_["fin_T"], b - 1)
                act.activation(outT_block[:, par, 0:n * P], outT[:, bass.ds(b * (BT * P), n * P)],
                               ACT.Copy).then_inc(S_["fin_copied"], 1)

            def finish_first():
                fin_copy(0, 0, BT, False)
                fin_copy(1, 1, BT, False)
                with act.Fori(1, EARLY // 2) as i:
                    for par in range(2):
                        fin_copy(i * 2 + par, par, BT, True)
                fin_copy(EARLY - 1, 0, BT, True)

            act.wait_ge(S_["early_ready"], 1)
            early = act.value_load(early_i[0:1, 0:1], min_val=0, max_val=1)
            for s in range(U):
                group_step(s, s, s, 0)
            group_turns(1, EARLY_TURN)
            with act.If(early > 0):
                group_turns(EARLY_TURN, EARLY_END, output=True)
            with act.Else():
                group_turns(EARLY_TURN, EARLY_END)
            group_turns(EARLY_END, R - 1)
            for s in range(NG - U, G_END):
                group_step(s, s, s, R - 1)

            act.wait_ge(S_["acc_done"], NG)
            with act.If(early < 1):
                finish_first()
            for b in range(EARLY, NB):
                fin_copy(b, b % 2, tiles_of(b), True)

        @block.tensor
        def _(pe):
            pe.wait_ge(S_["ident_ready"], 1)

            def columns(rows, half, name):
                for m in range(8):
                    k = 8 * half + m
                    i = pe.transpose(col_ps[half][:, m * R:(m + 1) * R], rows[:, k * P:(k + 1) * P], ident[0:R, 0:R])
                i.then_inc(S_[name], 1)


            def table_step(s):
                if 1 <= s <= NB:
                    b, par = s - 1, (s - 1) % 2
                    pe.wait_ge(S_["h_act"], b + 1)
                    if tiles_of(b) > PA:
                        pe.wait_ge(S_["h_pool"], b + 1)
                    wait(pe, "hT_done", b - 1, b - 1)
                    for t in range(tiles_of(b)):
                        i = pe.transpose(hT_ps[par][:, t * P:(t + 1) * P], h_sb[:, par, t, :], ident[:, :])
                    i.then_inc(S_["transp_done"], 1)
                if 2 <= s <= NB + 1:
                    b, par = s - 2, (s - 2) % 2
                    pe.wait_ge(S_["hT_done"], b + 1)
                    wait(pe, "q_evac", b - 1, b - 1)
                    wait(pe, "q_evac_act", b - 1, b - 1)
                    for t in range(tiles_of(b)):
                        i = pe.matmul((q_ps if t < QD else q_act_ps)[par][:, t * P:(t + 1) * P], hT_sb[:, b * BT + t, :], w1_sb[:, 1, :], start=True, stop=True)
                    i.then_inc(S_["q_done"], 1)

            pe.wait_ge(S_["weights_in"], 16)
            for s in range(T_END - 1):
                table_step(s)
                if s == 5:
                    pe.wait_ge(S_["src_f_ready"], 4)
                    for half in range(2):
                        columns(src_row_f, half, "src_T")
            pe.wait_ge(S_["wdiff_ready"], 1)
            pe.wait_ge(S_["q_evac_act"], NB - 1)
            for b in range(NB):
                wait(pe, "p_evac", b - 1, b - 1)
                for t in range(tiles_of(b)):
                    i = pe.matmul(p_ps[b % 2][:, t * P:(t + 1) * P], hT_sb[:, b * BT + t, :], w1_diff[:, :], start=True, stop=True)
                i.then_inc(S_["p_done"], 1)

            pe.wait_ge(S_["rel_last_ready"], 1)
            pe.wait_ge(S_["src_col_ready"], 2)
            for half in range(2):
                columns(rel_last, half, "rel_T")

            def broadcast_rel(c):
                pe.matmul(rel_ps[:, :], ones[:, :], rowbuf[:, c, 0, :], start=True, stop=True).then_inc(S_["rel_done"], 1)

            pe.wait_ge(S_["q_evac"], NB)
            pe.wait_ge(S_["p_evac"], NB)
            pe.wait_ge(S_["rel_col_ready"], 2)
            pe.wait_ge(S_["bias_in"], 48)

            def group_step(s, lo, hi, turn):
                c = lo % U
                if hi <= NG - 1:
                    missing = 0 if lo < NG - 1 else GT_ - LAST_TILES
                    pe.wait_ge(gathered[c], (turn + 1) * (16 * GT_) - 16 * missing)
                    wait(pe, "sum_done", s, lo)
                    for t in range(GT_ if lo < NG - 1 else LAST_TILES):
                        i = pe.transpose(GT_ps[:, t * P:(t + 1) * P], G[:, c, t, :], ident[:, :])
                    i.then_inc(S_["gt_done"], 1)
                    if lo == 0:
                        pe.wait_ge(row_in[0], 16)
                        broadcast_rel(0)
                    pe.wait_ge(win_in[c], (turn + 1) * 16)
                    pe.wait_ge(S_["onehot_done"], s + 1)
                    wait(pe, "px_evac", s, lo)
                    pe.matmul(PX_ps[:, :], p_win[:, c, :], onehot[:, lo % 2, :], start=True, stop=True).then_inc(S_["px_done"], 1)
                if hi + 1 <= NG - 1:
                    nxt = (lo + 1) % U
                    pe.wait_ge(row_in[nxt], (turn + 1 + (1 if nxt == 0 else 0)) * 16)
                    broadcast_rel(nxt)
                if lo >= 1 and hi - 1 <= NG - 1:
                    pe.wait_ge(S_["hidden_done"], s)
                    wait(pe, "m_evac", s - 1, lo - 1)
                    pe.matmul(M_ps[:, :], w2_sb[:, :], H[:, (lo - 1) % 2, :], start=True, stop=True).then_inc(S_["m_done"], 1)
                    wait(pe, "scan_done", s - 1, lo - 1)
                    pe.matmul(pen_ps[:, :], ones[:, :], rowbuf[:, (lo - 1) % U, 1, :],
                              start=True, stop=True).then_inc(S_["pen_done"], 1)
                if lo >= 2 and hi - 2 <= NG - 1:
                    pe.wait_ge(S_["scan_done"], s - 1)
                    wait(pe, "st_evac", s - 2, lo - 2)
                    for t in range(GT_):
                        i = pe.transpose(ST_ps[:, t * P:(t + 1) * P], S[:, (lo - 2) % 2, t * P:(t + 1) * P], ident[:, :])
                    i.then_inc(S_["st_done"], 1)
                if lo >= 3 and hi - 3 <= NG - 1:
                    pe.wait_ge(S_["st_evac"], s - 2)
                    pe.wait_ge(S_["L_done"], s - 2)
                    wait(pe, "acc_done", s - 3, lo - 3)
                    for t in range(GT_):
                        i = pe.matmul(sel_ps[:, 0:WN], ST[:, (lo - 3) % U, t, :], L[:, (lo - 3) % 2, t, :],
                                      start=(t == 0), stop=(t == GT_ - 1))
                    i.then_inc(S_["sel_done"], 1)

            def group_turns(first, end, output=False):
                with pe.Fori(first, end) as i:
                    for c in range(U):
                        group_step(i * U + c, U + c, (R - 2) * U + c, i)
                        if output and c == 2:
                            fin_transpose(early_ps, i - EARLY_TURN, 0, BT, False)
                        if output and c == U - 1:
                            pe.wait_ge(S_["fin_added"], i - (EARLY_TURN - 1))

            def fin_transpose(ps, b, par, n, again):
                pe.wait_ge(S_["fin_copied"], b + 1)
                if again:
                    pe.wait_ge(S_["fin_added"], b - 1)
                for t in range(n):
                    i = pe.transpose(ps[:, t * P:(t + 1) * P], outT_block[:, par, t * P:(t + 1) * P], ident[:, :])
                i.then_inc(S_["fin_T"], 1)

            def finish_first():
                fin_transpose(fin_ps[0], 0, 0, BT, False)
                fin_transpose(fin_ps[1], 1, 1, BT, False)
                with pe.Fori(1, EARLY // 2) as i:
                    for par in range(2):
                        fin_transpose(fin_ps[par], i * 2 + par, par, BT, True)
                fin_transpose(fin_ps[0], EARLY - 1, 0, BT, True)

            pe.wait_ge(S_["early_ready"], 1)
            early = pe.value_load(early_i[0:1, 0:1], min_val=0, max_val=1)
            for s in range(U):
                group_step(s, s, s, 0)
            group_turns(1, EARLY_TURN)
            with pe.If(early > 0):
                group_turns(EARLY_TURN, EARLY_END, output=True)
            with pe.Else():
                group_turns(EARLY_TURN, EARLY_END)
            group_turns(EARLY_END, R - 1)
            for s in range(NG - U, G_END):
                group_step(s, s, s, R - 1)

            with pe.If(early < 1):
                finish_first()
            for b in range(EARLY, NB):
                fin_transpose(fin_ps[b % 2], b, b % 2, tiles_of(b), True)

        @block.vector
        def _(dve):
            flat = lambda t: t[:, :, :].rearrange("r u e -> r (u e)")
            dve.memset(src_row[:, E_TAIL:RE], 0).then_inc(S_["edges_memset"], 1)
            dve.memset(flat(dst_row)[:, E_TAIL:RE], NO_NODE).then_inc(S_["edges_memset"], 1)
            dve.memset(flat(dst_next)[:, E_TAIL - 1:RE], NO_NODE).then_inc(S_["edges_memset"], 1)
            dve.memset(dst_before[:, :], -1).then_inc(S_["edges_memset"], 1)
            dve.memset(x_sb[:, NT - 1, :], 0.0).then_inc(S_["edges_memset"], 1)
            dve.memset(eps_col[:, :], EPS).then_inc(S_["dve_init"], 1)
            dve.memset(ones[:, :], 1.0).then_inc(S_["dve_init"], 1)
            dve.memset(end_row[:, NG - 1:NG], NO_NODE).then_inc(S_["dve_init"], 1)
            dve.wait_ge(S_["pool_init"], 4)
            dve.tensor_copy(iota_part[:, :], iota_part_i[:, :]).then_inc(S_["dve_init"], 1)
            dve.tensor_copy(iota_free1[:, :], iota_free_i[:, :]).then_inc(S_["dve_init"], 1)
            dve.memset(p_win[:, :, :], 0.0).then_inc(S_["loop_zeroed"], 1)

            def row_statistics(b):
                if b in X_CUTS:
                    k = X_CUTS.index(b)
                    dve.wait_ge(S_[f"x_in{k}"], 16 if k < 4 else 32)
                wait(dve, "mv_done", b - 1, b - 1)
                for t in range(tiles_of(b)):
                    i = dve.bn_stats(stats[:, b % 2, t, :], x_sb[:, b * BT + t, :])
                i.then_inc(S_["stats_done"], 1)

            def table_step(s):
                n, par = tiles_of(s), s % 2
                if s <= NB - 1:
                    dve.wait_ge(S_["stats_done"], s + 1)
                    wait(dve, "nm_done", s - 1, s - 1)
                    for t in range(n):
                        i = dve.bn_aggr(mean_var[:, par, t, :], stats[:, par, t, :])
                    i.then_inc(S_["mv_done"], 1)
                if s + 1 <= NB - 1:
                    row_statistics(s + 1)
                if s <= NB - 1:
                    dve.wait_ge(S_["sqrt_done"], s + 1)
                    wait(dve, "h_pool", s - 1, s - 1)
                    dve.reciprocal(rstd[:, par, 0:n], std[:, par, 0:n]).then_inc(S_["rstd_done"], 1)
                if 3 <= s <= NB + 2:
                    b = s - 3
                    m = tiles_of(b)
                    dve.wait_ge(S_["q_done"], b + 1)
                    if b < NB - 1:
                        m = QD
                        wait(dve, f"q_stored{b % 2}", b // 2 * 16, b // 2)
                        to = q_rows[:, b % 2, 0:QD, :].rearrange("p t n -> p (t n)")
                    else:
                        to = q_last[:, :]
                    dve.tensor_copy(to, q_ps[b % 2][:, 0:m * P]).then_inc(S_["q_evac"], 1)
                if s <= NB - 1:
                    dve.wait_ge(S_["rstd_done"], s + 1)
                    dve.scalar_tensor_tensor(neg_mean[:, par, 0:n], mean_var[:, par, 0:n, 0], -1.0, rstd[:, par, 0:n],
                                             ALU.mult, ALU.mult).then_inc(S_["nm_done"], 1)

            row_statistics(0)
            for s in range(T_END):
                table_step(s)

            dve.wait_ge(S_["base_in"], 32)
            dve.wait_ge(S_["dve_init"], 5)
            dve.tensor_tensor(wide_row[:, :], end_row[:, :], base_row[:, :], ALU.subtract).then_inc(S_["dve_small"], 1)
            dve.wait_ge(S_["dve_small"], 1)
            dve.tensor_scalar(end_row[:, :], wide_row[:, :], float(WN) - 0.5, None, ALU.is_ge).then_inc(S_["dve_small"], 1)
            dve.wait_ge(S_["dve_small"], 2)
            dve.reduce_max(any_wide_i[:, :], end_row[:, :], AX.X).then_inc(S_["anyw_ready"], 1)
            dve.wait_ge(S_["rel_i_ready"], 1)
            dve.tensor_scalar(wide[:, :], rel_i[:, :, GE - 1], float(WN) - 0.5, None, ALU.is_ge).then_inc(S_["wide_ready"], 1)
            dve.wait_ge(S_["wide_ready"], 1)
            dve.tensor_scalar(wide_off[:, :], wide[:, :], WIDE_OFF, None, ALU.mult).then_inc(S_["woff_ready"], 1)
            dve.wait_ge(S_["woff_ready"], 1)
            dve.tensor_tensor(rowpack[:, :, 0, :], rel_i[:, :, :],
                              wide_off[:, :].rearrange("r (u o) -> r u o", o=1).to_broadcast([R, U, GE]),
                              ALU.add).then_inc(S_["rel_row_ready"], 1)
            dve.wait_ge(S_["dst_in"], 32)
            dve.wait_ge(S_["dstn_in"], 32)
            dve.tensor_tensor(last[:, :].rearrange("r (u e) -> r u e", u=U), dst_row[:, :, :], dst_next[:, :, :],
                              ALU.not_equal).then_inc(S_["last_ready"], 1)
            dve.wait_ge(S_["before_in"], 16)
            dve.tensor_tensor(start[:, 0:1], dst_row[:, 0, 0:1], dst_before[:, :], ALU.not_equal).then_inc(S_["start_ready"], 1)
            dve.wait_ge(S_["last_ready"], 1)
            dve.tensor_scalar(rowpack[:, 0, 1, 1:GE], last[:, 0:GE - 1], PENALTY, None, ALU.mult)
            dve.tensor_scalar(rowpack[:, 1:U, 1, :], last[:, GE - 1:RE - 1].rearrange("r (u e) -> r u e", u=U - 1),
                              PENALTY, None, ALU.mult)
            dve.wait_ge(S_["start_ready"], 1)
            dve.tensor_scalar(rowpack[:, 0, 1, 0:1], start[:, 0:1], PENALTY, None, ALU.mult).then_inc(S_["pen_ready"], 1)
            dve.wait_ge(S_["rel_row_ready"], 1)
            dve.wait_ge(S_["src_T"], 2)
            dve.scalar_tensor_tensor(rel_last[:, :].rearrange("r (u e) -> r u e", u=U), rowpack[:, :, 0, :], 1.0,
                                     last[:, :].rearrange("r (u e) -> r u e", u=U), ALU.add, ALU.mult
                                     ).then_inc(S_["rel_last_ready"], 1)
            dve.tensor_scalar(block_end[:, :], iota_free1[0:1, 0:EARLY], float(BT * P), None, ALU.mult).then_inc(S_["dve_small"], 1)
            dve.wait_ge(S_["dve_small"], 3)
            first_groups = base_row[:, (EARLY_TURN - 1) * U:(EARLY_END - 1) * U].rearrange("o (t u) -> o t u", u=U)[:, :, 0]
            dve.tensor_tensor(short[:, :], block_end[:, :], first_groups, ALU.is_gt).then_inc(S_["dve_small"], 1)
            dve.wait_ge(S_["dve_small"], 4)
            dve.reduce_max(late[:, :], short[:, :], AX.X).then_inc(S_["dve_small"], 1)
            dve.wait_ge(S_["dve_small"], 5)
            dve.wait_ge(S_["anyw_ready"], 1)
            dve.tensor_tensor(late[:, :], late[:, :], any_wide_i[:, :], ALU.max).then_inc(S_["dve_small"], 1)
            dve.wait_ge(S_["dve_small"], 6)
            dve.tensor_scalar(early_i[:, :], late[:, :], 0.5, None, ALU.is_lt).then_inc(S_["early_ready"], 1)
            for half in range(2):
                dve.wait_ge(S_["rel_T"], half + 1)
                dve.tensor_copy(rel_last_col[:, :, 8 * half:8 * half + 8],
                                col_ps[half][:, 0:8 * R].rearrange("p (m r) -> p r m", m=8)).then_inc(S_["rel_col_ready"], 1)
            dve.wait_ge(S_["rel_col_ready"], 2)
            dve.wait_ge(S_["outT_zero"], 2)

            def one_hot(s, lo):
                dve.wait_ge(S_["rel_done"], s + 1)
                wait(dve, "px_done", s - 1, lo - 1)
                dve.tensor_scalar(onehot[:, lo % 2, :], rel_ps[:, :], iota_part[:, 0:1], None,
                                  ALU.is_equal).then_inc(S_["onehot_done"], 1)

            one_hot(0, 0)

            def group_step(s, lo, hi, turn):
                if hi <= NG - 1:
                    dve.wait_ge(S_["gt_done"], s + 1)
                    dve.wait_ge(S_["px_evac"], s + 1)
                    dve.tensor_tensor(px_sb[:, lo % 2, :], GT_ps[:, :], px_sb[:, lo % 2, :], ALU.add
                                      ).then_inc(S_["sum_done"], 1)
                if hi + 1 <= NG - 1:
                    one_hot(s + 1, lo + 1)
                if lo >= 2 and hi - 2 <= NG - 1:
                    wait(dve, "sel_done", s - 3, lo - 3)
                    row = (lo - 2) // U if lo == hi else (turn - 1 if lo % U < 2 else turn)
                    for t in range(GT_):
                        m = ((lo - 2) % U) * GT_ + t
                        i = dve.tensor_scalar(L[:, (lo - 2) % 2, t, :], iota_free1[:, 0:WN],
                                              rel_last_col[:, bass.ds(row, 1), m:m + 1].rearrange("p o t -> p (o t)"),
                                              None, ALU.is_equal)
                    i.then_inc(S_["L_done"], 1)
                if lo >= 1 and hi - 1 <= NG - 1:
                    dve.wait_ge(S_["m_evac"], s)
                    dve.wait_ge(S_["pen_done"], s)
                    wait(dve, "st_done", s - 2, lo - 2)
                    wait(dve, "scan_done", s - 1, lo - 1)
                    k = (lo - 1) % 2
                    initial = 0.0 if lo == 1 else S[:, 1 - k, GE - 1:GE]
                    dve.tensor_tensor_scan(S[:, k, :], pen_ps[:, :], M[:, k, :], initial, ALU.add, ALU.max
                                           ).then_inc(S_["scan_done"], 1)
                if lo >= 3 and hi - 3 <= NG - 1:
                    base = dve.value_load(base_row[0:1, bass.ds(s - 3, 1)], min_val=0, max_val=N - 1)
                    dve.wait_ge(S_["sel_done"], s - 2)
                    wait(dve, "acc_done", s - 3, lo - 3)
                    dve.tensor_tensor(outT[:, bass.ds(base, WN)], outT[:, bass.ds(base, WN)], sel_ps[:, 0:WN],
                                      ALU.add).then_inc(S_["acc_done"], 1)

            def group_turns(first, end, output=False):
                with dve.Fori(first, end) as i:
                    for c in range(U):
                        group_step(i * U + c, U + c, (R - 2) * U + c, i)
                        if output and c == 2:
                            fin_add(early_ps, i - EARLY_TURN, BT)

            def fin_add(ps, b, n):
                dve.wait_ge(S_["fin_T"], b + 1)
                tiles = x_sb[:, bass.ds(b * BT, n), :].rearrange("p t f -> p (t f)")
                dve.tensor_tensor(tiles, tiles, ps[:, 0:n * P], ALU.add).then_inc(S_["fin_added"], 1)

            def finish_first():
                with dve.Fori(0, EARLY // 2) as i:
                    for par in range(2):
                        fin_add(fin_ps[par], i * 2 + par, BT)
                fin_add(fin_ps[0], EARLY - 1, BT)

            dve.wait_ge(S_["early_ready"], 1)
            early = dve.value_load(early_i[0:1, 0:1], min_val=0, max_val=1)
            for s in range(U):
                group_step(s, s, s, 0)
            group_turns(1, EARLY_TURN)
            with dve.If(early > 0):
                group_turns(EARLY_TURN, EARLY_END, output=True)
            with dve.Else():
                group_turns(EARLY_TURN, EARLY_END)
            group_turns(EARLY_END, R - 1)
            for s in range(NG - U, G_END):
                group_step(s, s, s, R - 1)

            dve.wait_ge(S_["wide_merged"], 1)
            with dve.If(early < 1):
                finish_first()
            for b in range(EARLY, NB):
                fin_add(fin_ps[b % 2], b, tiles_of(b))


_INS = ['x', 'src', 'dst', 'L0_gnn_W1', 'L0_gnn_b1', 'L0_gnn_W2', 'L0_gnn_b2']


def kernel(**inputs):
    import numpy as _np
    import concourse.bacc as _bacc
    from concourse import mybir as _mybir
    from concourse.bass_utils import run_bass_kernel_spmd as _run

    nc = _bacc.Bacc("TRN2", target_bir_lowering=False, num_devices=1)
    arrays, args = {}, []
    for name in _INS:
        a = _np.ascontiguousarray(inputs[name])
        arrays[f"in_{name}_dram"] = a
        args.append(nc.dram_tensor(f"in_{name}_dram", a.shape, _mybir.dt.from_np(a.dtype), kind="ExternalInput").ap())
    shape = inputs["x"].shape
    args.append(nc.dram_tensor("out_0_dram", shape, _mybir.dt.float32, kind="ExternalOutput").ap())
    gnn_kernel(nc, *args)
    r = _run(nc, [arrays], core_ids=[0])
    return r.results[0]["out_0_dram"]
```
